# Optimizing a Trainium2 kernel written in Bass

```python
import numpy as np
import jax
import jax.numpy as jnp

def _softmax(x, axis=-1):
    return jax.nn.softmax(x, axis=axis)

def _gelu(x):
    return jax.nn.gelu(x, approximate=True)

def _silu(x):
    return jax.nn.silu(x)

def _sigmoid(x):
    return jax.nn.sigmoid(x)

def _layernorm(x, axis=-1, eps=1e-05):
    m = jnp.mean(x, axis=axis, keepdims=True)
    v = jnp.var(x, axis=axis, keepdims=True)
    return (x - m) / jnp.sqrt(v + eps)

def _scatter_add(tgt, idx, src, axis=0):
    return tgt.at[idx].add(src)

def _segment_sum(src, seg, n):
    return jax.ops.segment_sum(src, seg, n)
kernel_name = 'mk_decoder_postln_d1_seqx_r4_d68436'

def setup_inputs(seed: int=0):
    np.random.seed(seed)
    _w = jnp.asarray

    def _rec_inputs():
        import jax
        import jax.numpy as jnp
        _rk = jax.random.key(seed)
        x = 7.22e-05 + 1 * jax.random.normal(jax.random.fold_in(_rk, 1), (128, 128, 256), jnp.float32)
        _lenS = 128 - jax.random.randint(jax.random.fold_in(_rk, 7), (128,), 0, max(1, 128 // 4) + 1, jnp.int32)
        _lenS2 = 128 - jax.random.randint(jax.random.fold_in(_rk, 8), (128,), 0, max(1, 128 // 4) + 1, jnp.int32)
        _ctx_1024P = jax.random.normal(jax.random.fold_in(_rk, 11), (128, 16, 256), jnp.float32)
        _ctx_1024c = jax.random.dirichlet(jax.random.fold_in(_rk, 511), 0.3 * jnp.ones((16,), jnp.float32), (128, 128))
        _ctx_1024t = jnp.einsum('bsk,bkd->bsd', _ctx_1024c, _ctx_1024P)
        _ctx_1024t = _ctx_1024t * jax.lax.rsqrt(jnp.mean(jnp.square(_ctx_1024t)) + 1e-12) * 0.953939
        ctx_1024 = 4.13588e-05 + 0.999923 * (_ctx_1024t + 0.3 * jax.random.normal(jax.random.fold_in(_rk, 611), (128, 128, 256), jnp.float32))
        _validS = jnp.arange(128)[None, :] < _lenS[:, None]
        _validS2 = jnp.arange(128)[None, :] < _lenS2[:, None]
        _causal = jnp.tril(jnp.ones((128, 128), dtype=bool))
        mask_BxSxS2_ik1 = jnp.where(jnp.broadcast_to(_validS2[:, None, :], (128, 128, 128)), 1, 0).astype(jnp.int32)
        return (x, ctx_1024, mask_BxSxS2_ik1)
    x, ctx_1024, mask_BxSxS2_ik1 = _rec_inputs()

    def _L0_attn_setup():
        import jax, jax.numpy as jnp
        import numpy as np
        import math
        B, T, C = (4, 512, 256)
        H, DQK, DV = (16, 64, 64)
        key = jax.random.key(seed)
        k1, k2, k3, k4, k5 = jax.random.split(key, 5)
        x_q = jax.random.normal(k1, (B, T, C), dtype=jnp.float32)
        w_q = jax.random.normal(k2, (H, DQK, C), dtype=jnp.float32) / math.sqrt(C)
        w_k = jax.random.normal(k3, (H, DQK, C), dtype=jnp.float32) / math.sqrt(C)
        w_v = jax.random.normal(k4, (H, DV, C), dtype=jnp.float32) / math.sqrt(C)
        w_o = jax.random.normal(k5, (DV * H, C), dtype=jnp.float32) / math.sqrt(C)
        return {'x_q': x_q, 'w_q': w_q, 'w_k': w_k, 'w_v': w_v, 'w_o': w_o}
    _L0_attn_all = _L0_attn_setup()
    _L0_attn_in = {k: v for k, v in _L0_attn_all.items() if k in ('w_q', 'w_k', 'w_v', 'w_o')}
    del _L0_attn_all

    def _L0_xattn_setup():
        import jax, jax.numpy as jnp
        import numpy as np
        H = 16
        D_MODEL = 256
        DK = D_MODEL // H
        NEG = -1000000000.0

        def _split_heads(x, B, S):
            return x.reshape(B, S, H, DK).transpose(0, 2, 1, 3)
        key = jax.random.key(seed)
        ks = jax.random.split(key, 13)
        B, S, D = (4, 512, D_MODEL)
        scale = 1.0 / np.sqrt(D)
        inp = {'q': jax.random.normal(ks[0], (B, S, D), jnp.float32), 'k': jax.random.normal(ks[1], (B, S, D), jnp.float32), 'v': jax.random.normal(ks[2], (B, S, D), jnp.float32), 'mask': jax.random.randint(ks[3], (B, S, S), 0, 2, jnp.int32), 'Wq': jax.random.normal(ks[4], (D, D), jnp.float32) * scale, 'bq': jnp.zeros((D,), jnp.float32), 'Wk': jax.random.normal(ks[5], (D, D), jnp.float32) * scale, 'bk': jnp.zeros((D,), jnp.float32), 'Wv': jax.random.normal(ks[6], (D, D), jnp.float32) * scale, 'bv': jnp.zeros((D,), jnp.float32), 'Wo': jax.random.normal(ks[7], (D, D), jnp.float32) * scale, 'bo': jnp.zeros((D,), jnp.float32)}
        return inp
    _L0_xattn_all = _L0_xattn_setup()
    _L0_xattn_in = {k: v for k, v in _L0_xattn_all.items() if k in ('Wq', 'bq', 'Wk', 'bk', 'Wv', 'bv', 'Wo', 'bo')}
    del _L0_xattn_all

    def _L0_ffn_setup():
        import jax, jax.numpy as jnp
        from jax import lax
        import numpy as np
        D_MODEL = 256
        HIDDEN = 128
        N_EXPERTS = 32
        TOP_K = 2
        B, S = (1, 1024)

        def _moe_group(x2, router_w, wg, wu, wd, top_k):
            T = x2.shape[0]
            n_experts = router_w.shape[1]
            logits = x2 @ router_w
            scores = jax.nn.softmax(logits, axis=-1)
            expert_weights, expert_indices = lax.top_k(scores, top_k)
            flat_e = expert_indices.reshape(-1)
            flat_w = expert_weights.reshape(-1)
            flat_t = jnp.repeat(jnp.arange(T), top_k)
            order = jnp.argsort(flat_e)
            tok = flat_t[order]
            xs = x2[tok]
            group_sizes = jnp.bincount(flat_e, length=n_experts).astype(jnp.int32)
            gate = lax.ragged_dot(xs, wg, group_sizes)
            up = lax.ragged_dot(xs, wu, group_sizes)
            ys = lax.ragged_dot(jax.nn.silu(gate) * up, wd, group_sizes)
            ys = ys * flat_w[order][:, None]
            return jnp.zeros_like(x2).at[tok].add(ys)
        key = jax.random.key(seed)
        ks = jax.random.split(key, 9)
        w = lambda k, shape: jax.random.normal(k, shape, dtype=jnp.float32) * 0.02
        return {'x': jax.random.normal(ks[0], (B, S, D_MODEL), dtype=jnp.float32), 'router_w0': w(ks[1], (D_MODEL, N_EXPERTS)), 'wg0': w(ks[2], (N_EXPERTS, D_MODEL, HIDDEN)), 'wu0': w(ks[3], (N_EXPERTS, D_MODEL, HIDDEN)), 'wd0': w(ks[4], (N_EXPERTS, HIDDEN, D_MODEL)), 'router_w1': w(ks[5], (D_MODEL, N_EXPERTS)), 'wg1': w(ks[6], (N_EXPERTS, D_MODEL, HIDDEN)), 'wu1': w(ks[7], (N_EXPERTS, D_MODEL, HIDDEN)), 'wd1': w(ks[8], (N_EXPERTS, HIDDEN, D_MODEL))}
    _L0_ffn_all = _L0_ffn_setup()
    _L0_ffn_in = {k: v for k, v in _L0_ffn_all.items() if k in ('router_w0', 'wg0', 'wu0', 'wd0', 'router_w1', 'wg1', 'wu1', 'wd1')}
    del _L0_ffn_all
    return {'x': x, 'ctx_1024': ctx_1024, 'mask_BxSxS2_ik1': mask_BxSxS2_ik1, 'L0_attn_w_q': _L0_attn_in['w_q'], 'L0_attn_w_k': _L0_attn_in['w_k'], 'L0_attn_w_v': _L0_attn_in['w_v'], 'L0_attn_w_o': _L0_attn_in['w_o'], 'L0_xattn_Wq': _L0_xattn_in['Wq'], 'L0_xattn_bq': _L0_xattn_in['bq'], 'L0_xattn_Wk': _L0_xattn_in['Wk'], 'L0_xattn_bk': _L0_xattn_in['bk'], 'L0_xattn_Wv': _L0_xattn_in['Wv'], 'L0_xattn_bv': _L0_xattn_in['bv'], 'L0_xattn_Wo': _L0_xattn_in['Wo'], 'L0_xattn_bo': _L0_xattn_in['bo'], 'L0_ffn_router_w0': _L0_ffn_in['router_w0'], 'L0_ffn_wg0': _L0_ffn_in['wg0'], 'L0_ffn_wu0': _L0_ffn_in['wu0'], 'L0_ffn_wd0': _L0_ffn_in['wd0'], 'L0_ffn_router_w1': _L0_ffn_in['router_w1'], 'L0_ffn_wg1': _L0_ffn_in['wg1'], 'L0_ffn_wu1': _L0_ffn_in['wu1'], 'L0_ffn_wd1': _L0_ffn_in['wd1']}

def reference(x, ctx_1024, mask_BxSxS2_ik1, L0_attn_w_q, L0_attn_w_k, L0_attn_w_v, L0_attn_w_o, L0_xattn_Wq, L0_xattn_bq, L0_xattn_Wk, L0_xattn_bk, L0_xattn_Wv, L0_xattn_bv, L0_xattn_Wo, L0_xattn_bo, L0_ffn_router_w0, L0_ffn_wg0, L0_ffn_wu0, L0_ffn_wd0, L0_ffn_router_w1, L0_ffn_wg1, L0_ffn_wu1, L0_ffn_wd1):
    import jax
    import jax.numpy as jnp

    def _L0_attn_ref(x_q, w_q, w_k, w_v, w_o):
        import jax, jax.numpy as jnp
        import numpy as np
        import math
        B, T, C = (4, 512, 256)
        H, DQK, DV = (16, 64, 64)
        q = jnp.einsum('ntc,hdc->nhtd', x_q, w_q)
        k = jnp.einsum('ntc,hdc->nhtd', x_q, w_k)
        v = jnp.einsum('ntc,hdc->nhtd', x_q, w_v)
        a = jnp.einsum('nhtd,nhsd->nhts', q, k) / math.sqrt(q.shape[3])
        t = a.shape[2]
        causal_forbidden = jnp.arange(t)[:, None] < jnp.arange(t)[None, :]
        a = jnp.where(causal_forbidden[None, None], -jnp.inf, a)
        a = jax.nn.softmax(a, axis=3)
        y = jnp.einsum('nhts,nhsd->nthd', a, v).reshape(a.shape[0], t, -1)
        return y @ w_o

    def _L0_xattn_ref(q, k, v, mask, Wq, bq, Wk, bk, Wv, bv, Wo, bo):
        import jax, jax.numpy as jnp
        import numpy as np
        H = 16
        D_MODEL = 256
        DK = D_MODEL // H
        NEG = -1000000000.0

        def _split_heads(x, B, S):
            return x.reshape(B, S, H, DK).transpose(0, 2, 1, 3)
        B, S, D = q.shape
        qh = _split_heads(q @ Wq.T + bq, B, S)
        kh = _split_heads(k @ Wk.T + bk, B, S)
        vh = _split_heads(v @ Wv.T + bv, B, S)
        scores = jnp.einsum('bhqd,bhkd->bhqk', qh, kh) / np.sqrt(DK)
        scores = jnp.where(mask[:, None, :, :] == 0, NEG, scores)
        attn = jax.nn.softmax(scores, axis=-1)
        out = jnp.einsum('bhqk,bhkd->bhqd', attn, vh)
        out = out.transpose(0, 2, 1, 3).reshape(B, S, D)
        return out @ Wo.T + bo

    def _L0_ffn_ref(x, router_w0, wg0, wu0, wd0, router_w1, wg1, wu1, wd1):
        import jax, jax.numpy as jnp
        from jax import lax
        import numpy as np
        D_MODEL = 256
        HIDDEN = 128
        N_EXPERTS = 32
        TOP_K = 2
        B, S = (1, 1024)

        def _moe_group(x2, router_w, wg, wu, wd, top_k):
            T = x2.shape[0]
            n_experts = router_w.shape[1]
            logits = x2 @ router_w
            scores = jax.nn.softmax(logits, axis=-1)
            expert_weights, expert_indices = lax.top_k(scores, top_k)
            flat_e = expert_indices.reshape(-1)
            flat_w = expert_weights.reshape(-1)
            flat_t = jnp.repeat(jnp.arange(T), top_k)
            order = jnp.argsort(flat_e)
            tok = flat_t[order]
            xs = x2[tok]
            group_sizes = jnp.bincount(flat_e, length=n_experts).astype(jnp.int32)
            gate = lax.ragged_dot(xs, wg, group_sizes)
            up = lax.ragged_dot(xs, wu, group_sizes)
            ys = lax.ragged_dot(jax.nn.silu(gate) * up, wd, group_sizes)
            ys = ys * flat_w[order][:, None]
            return jnp.zeros_like(x2).at[tok].add(ys)
        b, s, d = x.shape
        x2 = x.reshape(-1, d)
        out0 = _moe_group(x2, router_w0, wg0, wu0, wd0, TOP_K)
        out1 = _moe_group(x2, router_w1, wg1, wu1, wd1, TOP_K)
        out = (out0 * TOP_K + out1 * TOP_K) / (TOP_K + TOP_K)
        return out.reshape(b, s, d)
    x = _layernorm(x + _L0_attn_ref(x, L0_attn_w_q, L0_attn_w_k, L0_attn_w_v, L0_attn_w_o), axis=-1)
    x = _layernorm(x + _L0_xattn_ref(x, ctx_1024, ctx_1024, mask_BxSxS2_ik1, L0_xattn_Wq, L0_xattn_bq, L0_xattn_Wk, L0_xattn_bk, L0_xattn_Wv, L0_xattn_bv, L0_xattn_Wo, L0_xattn_bo), axis=-1)
    x = _layernorm(x + _L0_ffn_ref(x, L0_ffn_router_w0, L0_ffn_wg0, L0_ffn_wu0, L0_ffn_wd0, L0_ffn_router_w1, L0_ffn_wg1, L0_ffn_wu1, L0_ffn_wd1), axis=-1)
    return x

_drawn_inputs = setup_inputs


def setup_inputs(seed=0):
    import zlib

    import numpy as np

    out = dict(_drawn_inputs(seed))
    spreads = {'L0_xattn_bq': (0.0, 0.375),
     'L0_xattn_bk': (0.0, 0.8),
     'L0_xattn_bv': (0.0, 0.1),
     'L0_xattn_bo': (0.0, 0.1)}
    factors = {'L0_ffn_router_w0': 8.0,
     'L0_ffn_wg0': 8.0,
     'L0_ffn_wu0': 8.0,
     'L0_ffn_wd0': 8.0,
     'L0_ffn_router_w1': 8.0,
     'L0_ffn_wg1': 8.0,
     'L0_ffn_wu1': 8.0,
     'L0_ffn_wd1': 8.0}
    for name, (base, spread) in spreads.items():
        noise = np.random.default_rng([zlib.crc32(name.encode()), seed]).standard_normal(out[name].shape)
        drawn = base * np.exp(spread * noise) if base else spread * noise
        out[name] = jnp.asarray(drawn.astype(out[name].dtype))
    for name, factor in factors.items():
        out[name] = (out[name] * factor).astype(out[name].dtype)
    return out
```

```python
from contextlib import ExitStack

import concourse.bass as bass
from concourse import mybir

F32 = mybir.dt.float32
BF16 = mybir.dt.bfloat16
I32 = mybir.dt.int32
U32 = mybir.dt.uint32
ALU = mybir.AluOpType
ACT = mybir.ActivationFunctionType
AX = mybir.AxisListType

P = 128
D = 256
KC = D // P
H, DH = 16, 64
HD = H * DH
PAIRS = H // 2
XH = 16
XD = D // XH
XPC = P // XD
QUARTERS = XPC // 2
GH = 4
NG = H // GH
E, TOPK, NGRP = 32, 2, 2
NE = E * NGRP
HID = 128
WCOL = KC * 2 * HID + D
HALF = E // 2
EPS = 1e-5
BIG = float(2.0 ** 100)
RSQRT_SEED = float(0x5F3759DF)
SLOTS = NGRP * TOPK


class When:

    def __init__(self, u, p, n, first, last):
        self.u, self.p, self.n, self.first, self.last = u, p, n, first, last

    def live(self, lag):
        return not isinstance(self.u, int) or self.first <= self.n * self.u + self.p - lag < self.last

    def item(self, lag):
        return self.u * self.n + (self.p - lag)

    def slot(self, lag):
        return (self.p - lag) % self.n

    def turn(self, lag):
        return self.u + (self.p - lag) // self.n


def at(number, n, first, last):
    return When(number // n, number % n, n, first, last)


def wait(eng, sem, value):
    if isinstance(value, int) and value <= 0:
        return
    eng.wait_ge(sem, value)


def settle(eng, settled):
    eng.sem_inc(settled, 1)


class Steps:

    def __init__(self, eng, sem, size, item):
        self.eng, self.sem, self.base, self.size, self.n = eng, sem, item * size, size, 0

    def done(self, instruction):
        self.n += 1
        assert self.n <= self.size
        instruction.then_inc(self.sem, 1)

    def need(self, n=None):
        self.eng.wait_ge(self.sem, self.base + (self.n if n is None else n))


def spread(ap, axis, n):
    a = ap.unsqueeze(axis)
    shape = list(a.shape)
    shape[axis] = n
    return a.broadcast_to(shape)


JOBS = [
    (0, "q0", -1, 0), (0, "q1", -1, 0),
    (1, "o2", 3, 0), (1, "rank", 4, D), (1, "o1", 1, 0),
    (2, "k0", -1, 0), (2, "k1", -1, 0), (2, "xk", 1, 0), (2, "x1t", 1, 0), (2, "x2t", 3, D),
    (3, "v0", -1, 0), (3, "xq", 1, 0), (3, "route", 3, D), (3, "v1", -1, 0), (3, "xv", 1, 0),
]
JBANKS = 3
USE = [sum(1 for _, _, _, c in JOBS[:n + 1] if c == 0) - 1 for n in range(len(JOBS))]
USES = USE[-1] + 1
BANK = {job[1]: USE[n] % JBANKS for n, job in enumerate(JOBS)}
MOVES = {"k0": 2, "k1": 2}
assert USES % JBANKS == 0


def bank_before(t, n):
    for use in range(USE[n] - JBANKS, USE[n] - 4 * USES, -JBANKS):
        back = -(use // USES)
        found = [(name, t.item(lag + back) + 1) for m, (_, name, lag, _) in enumerate(JOBS)
                 if USE[m] == use % USES and t.live(lag + back)]
        if found:
            return found
    return []


def decoder_layer(nc, xT, x, cT, mask, wq, wk, wv, wo, xwq, xbq, xwk, xbk, xwv, xbv, xwo, xbo,
                  r0, g0, u0, d0, r1, g1, u1, d1, out):
    NB = x.shape[0]
    N = NB * P
    TILES = NB * TOPK + E
    NT = NGRP * TILES
    TA = -(-NT // P)
    x2_d = nc.dram_tensor("x2_d", (N, D), F32).ap()
    list_d = nc.dram_tensor("list_d", (NE * N, 1), I32).ap()
    y_d = nc.dram_tensor("y_d", (NT * P, D), F32).ap()
    tab_d = nc.dram_tensor("tab_d", (TA * P,), I32).ap()

    keep = ExitStack()
    with keep:
        def tile(stack, name, shape, dt=F32):
            return stack.enter_context(nc.sbuf_tensor(name, shape, dt))

        def sem(name):
            return keep.enter_context(nc.semaphore(name))

        banks = [keep.enter_context(nc.psum_tensor(f"bank{i}", [P, 512], F32)) for i in range(8)]

        ident = tile(keep, "ident", [P, P])
        ones_b = tile(keep, "ones_b", [P, P], BF16)
        picked = tile(keep, "picked", [P, NE], BF16)
        expert = tile(keep, "expert", [P, NB, SLOTS])
        rank = tile(keep, "rank", [P, NB, SLOTS])
        weight = tile(keep, "weight", [P, NB, SLOTS])
        row_i = tile(keep, "row_i", [P, NB, SLOTS], I32)

        settled = sem("settled")

        def load_experts(eng, dst, first, gate, up, down, done):
            for k in range(KC):
                for j, w in enumerate((gate, up)):
                    eng.dma_start(dst[:, :, (2 * k + j) * HID:(2 * k + j + 1) * HID],
                                  w[first:first + HALF, k * P:(k + 1) * P, :].rearrange("e p h -> p e h")).then_inc(done, 16)
            eng.dma_start(dst[:, :, KC * 2 * HID:WCOL],
                          down[first:first + HALF, :, :].rearrange("e p d -> p e d")).then_inc(done, 16)

        MOE_LOAD = 16 * (2 * KC + 1)
        RSQRT_STEPS = 12

        def newton(steps, tiles, turns):
            var, ve, bits, y, a, b = tiles
            v = nc.vector
            for _ in range(turns):
                steps.need()
                steps.done(v.tensor_tensor(a, y, y, ALU.mult))
                steps.need()
                steps.done(v.scalar_tensor_tensor(b, a, -0.5, ve, ALU.mult, ALU.mult))
                steps.need()
                steps.done(v.scalar_tensor_tensor(y, b, 1.5, y, ALU.add, ALU.mult))

        def rsqrt_begin(steps, tiles):
            var, ve, bits, y, a, b = tiles
            v = nc.vector
            steps.done(v.tensor_scalar(ve, var, EPS, None, ALU.add))
            steps.need()
            steps.done(v.tensor_single_scalar(bits.bitcast(I32), ve.bitcast(I32), 1, op=ALU.arith_shift_right))
            steps.need()
            steps.done(v.tensor_scalar(y.bitcast(I32), bits.bitcast(I32), -1.0, RSQRT_SEED, ALU.mult, ALU.add))
            newton(steps, tiles, 1)

        def rsqrt_end(steps, tiles):
            newton(steps, tiles, 2)

        with ExitStack() as one:
            def sb(name, shape, dt=F32):
                return tile(one, name, shape, dt)

            wq_s, wk_s, wv_s = (sb(n, [P, KC, HD]) for n in ("wq_s", "wk_s", "wv_s"))
            wo_s = sb("wo_s", [P, PAIRS, D])
            xwq_s, xwk_s, xwv_s, xwo_s = (sb(n, [P, KC, D]) for n in ("xwq_s", "xwk_s", "xwv_s", "xwo_s"))
            xbq_s, xbk_s = sb("xbq_s", [P, KC]), sb("xbk_s", [P, KC])
            bias_row = sb("bias_row", [1, 2, D])
            xbv_s, xbo_s = sb("xbv_s", [P, D]), sb("xbo_s", [P, D])
            router_s = sb("router_s", [P, KC, NE])
            ident_b = sb("ident_b", [P, P], BF16)
            causal_b = sb("causal_b", [P, P], BF16)
            before_b = sb("before_b", [P, P], BF16)
            own_head = sb("own_head", [P, XPC])
            iota_e = sb("iota_e", [P, E])
            group_first = sb("group_first", [P, SLOTS])
            token_no = sb("token_no", [P, NB], I32)
            zeros = sb("zeros", [P, 512], I32)

            xT_s = [sb(f"xT{p}", [P, KC, P]) for p in (0, 1)]
            x_s = [sb(f"x{p}", [P, D]) for p in (0, 1)]
            cT_s = [sb(f"cT{p}", [P, KC, P]) for p in (0, 1)]
            mask_s = [sb(f"mask{p}", [P, P], I32) for p in (0, 1)]
            xmask_b = [sb(f"xmask{p}", [P, P], BF16) for p in (0, 1)]
            qT = [sb(f"qT{p}", [P, PAIRS, P]) for p in (0, 1)]
            kD = [sb(f"kD{p}", [P, PAIRS, 2 * P]) for p in (0, 1)]
            v_s = [sb(f"v{p}", [P, HD]) for p in (0, 1)]
            xqT = [sb(f"xqT{p}", [P, KC, P]) for p in (0, 1)]
            xkD = [sb(f"xkD{p}", [P, KC, XPC, P]) for p in (0, 1)]
            xvD = [sb(f"xvD{p}", [P, KC, QUARTERS, 2, 2 * XD]) for p in (0, 1)]
            prob = [sb(f"prob{p}", [P, GH, P]) for p in (0, 1)]
            xprob = [sb(f"xprob{p}", [P, GH, P]) for p in (0, 1)]
            probT, xprobT = sb("probT", [P, GH, P]), sb("xprobT", [P, GH, P])
            negmax = [sb(f"negmax{p}", [P, GH]) for p in (0, 1)]
            xnegmax = [sb(f"xnegmax{p}", [P, GH]) for p in (0, 1)]
            total = [sb(f"total{p}", [P, GH]) for p in (0, 1)]
            xtotal = [sb(f"xtotal{p}", [P, GH]) for p in (0, 1)]
            inv, xinv = sb("inv", [P, GH]), sb("xinv", [P, GH])
            yT, xyT = sb("yT", [P, PAIRS, P]), sb("xyT", [P, KC, P])
            sum1, sum2 = sb("sum1", [P, D]), sb("sum2", [P, D])
            stats, mv = sb("stats", [P, 2, 6]), sb("mv", [P, 2, 2])
            rs = sb("rs", [P, 2, 5])
            x1 = [sb(f"x1_{p}", [P, D]) for p in (0, 1)]
            x1b = [sb(f"x1b_{p}", [P, D]) for p in (0, 1)]
            x2 = [sb(f"x2_{p}", [P, D]) for p in (0, 1)]
            x1T, x2T = sb("x1T", [P, KC, P]), sb("x2T", [P, KC, P])
            top8, top8i = sb("top8", [P, NGRP, 8]), sb("top8i", [P, NGRP, 8], U32)
            below = sb("below", [P, NE + NGRP])
            soft = sb("soft", [P, NE + NGRP])
            soft_sum, soft_inv = sb("soft_sum", [P, NGRP]), sb("soft_inv", [P, NGRP])
            choice = sb("choice", [P, NGRP, TOPK])
            hot = sb("hot", [P, NGRP, TOPK, E])
            hot_b = sb("hot_b", [P, NGRP, E], BF16)
            hot_rank = sb("hot_rank", [P, NGRP, TOPK, E])
            list_row = sb("list_row", [P, SLOTS])
            place = [sb(f"place{p}", [P, SLOTS], I32) for p in (0, 1)]
            token = [sb(f"token{p}", [P, 1], I32) for p in (0, 1)]

            S, XS, T, XT, PV, JB = banks[0], banks[1], banks[2], banks[3], banks[4], banks[5:8]
            SELF, CROSS = slice(0, 2 * P), slice(2 * P, 3 * P)

            weights_in = sem("weights_in")
            consts = sem("consts")
            zeroed = sem("zeroed")
            list_clear = sem("list_clear")
            xT_in, x_in, cT_in, mask_in = ([sem(f"{n}_in{p}") for p in (0, 1)] for n in ("xT", "x", "cT", "mask"))
            x2_out = [sem(f"x2_out{p}") for p in (0, 1)]
            placed = [sem(f"placed{p}") for p in (0, 1)]
            scores, xscores = sem("scores"), sem("xscores")
            maxed, xmaxed = sem("maxed"), sem("xmaxed")
            exped, xexped = sem("exped"), sem("xexped")
            normed, xnormed = sem("normed"), sem("xnormed")
            turned, xturned = sem("turned"), sem("xturned")
            probT_in, xprobT_in = sem("probT_in"), sem("xprobT_in")
            mixed, xmixed = sem("mixed"), sem("xmixed")
            yT_in, xyT_in = sem("yT_in"), sem("xyT_in")
            made = {n: sem(f"made_{n}") for _, n, _, _ in JOBS}
            moved = {n: sem(f"moved_{n}") for _, n, _, _ in JOBS}
            x1_ready, x1b_ready, x2_ready = sem("x1_ready"), sem("x1b_ready"), sem("x2_ready")
            xmask_ready = sem("xmask_ready")
            soft_ready = sem("soft_ready")
            hot_ready, picked_ready = sem("hot_ready"), sem("picked_ready")
            place_ready, list_row_ready = sem("place_ready"), sem("list_row_ready")
            inv_ready, xinv_ready = sem("inv_ready"), sem("xinv_ready")
            place_step, norm1_step, norm2_step, rsqrt_step, route_step, weigh_step = (
                sem(n) for n in ("place_step", "norm1_step", "norm2_step", "rsqrt_step", "route_step", "weigh_step"))

            W_IN = 16 * 16

            def pipeline(eng, iteration):
                for i in range(-1, 6):
                    iteration(at(i, 2, 0, NB))
                with eng.Fori(3, NB // 2 - 1) as u:
                    for p in (0, 1):
                        iteration(When(u, p, 2, 0, NB))
                for i in range(NB - 2, NB + 4):
                    iteration(at(i, 2, 0, NB))

            def behind(s, lag):
                return (lag, s - 1) if s else (lag + 1, NG - 1)

            with nc.Block() as block:
                @block.sync
                def _(sp):
                    sp.dma_start(xT_s[0][:, :, :].rearrange("p k t -> p (k t)"), xT[0, :, :]).then_inc(xT_in[0], 16)
                    for dst, src in ((wq_s, wq), (wk_s, wk), (wv_s, wv), (wo_s, wo), (xwq_s, xwq), (xwk_s, xwk),
                                     (xwv_s, xwv), (xwo_s, xwo)):
                        sp.dma_start(dst[:, :, :].rearrange("p k n -> p (k n)"), src).then_inc(weights_in, 16)
                    for dst, src in ((xbq_s[:, :], xbq), (xbk_s[:, :], xbk)):
                        sp.dma_start(dst, src).then_inc(weights_in, 16)
                    sp.dma_start(bias_row[0:1, 0, :], xbv).then_inc(weights_in, 16)
                    sp.dma_start(bias_row[0:1, 1, :], xbo).then_inc(weights_in, 16)
                    for k in range(KC):
                        for g, r in enumerate((r0, r1)):
                            sp.dma_start(router_s[:, k, g * E:(g + 1) * E], r[k * P:(k + 1) * P, :]).then_inc(weights_in, 16)
                    sp.wait_ge(zeroed, 1)
                    clear = list_d.rearrange("(c p n) o -> c p (n o)", p=P, n=min(512, NE * N // P))
                    for c in range(clear.shape[0]):
                        sp.dma_start(clear[c, :, :], zeros[:, 0:clear.shape[2]]).then_inc(list_clear, 16)

                    def iteration(t):
                        if t.live(-2):
                            wait(sp, made["v1"], t.item(0) + 1)
                            sp.dma_start(xT_s[t.slot(-2)][:, :, :].rearrange("p k t -> p (k t)"),
                                         xT[bass.ds(t.item(-2), 1), :, :].rearrange("o p n -> (o p) n")).then_inc(xT_in[t.slot(-2)], 16)
                        if t.live(0):
                            wait(sp, made["xv"], t.item(2) + 1)
                            sp.dma_start(cT_s[t.slot(0)][:, :, :].rearrange("p k t -> p (k t)"),
                                         cT[bass.ds(t.item(0), 1), :, :].rearrange("o p n -> (o p) n")).then_inc(cT_in[t.slot(0)], 16)
                            wait(sp, xmask_ready, t.item(2) + 1)
                            sp.dma_start(mask_s[t.slot(0)][:, :],
                                         mask[bass.ds(t.item(0), 1), :, :].rearrange("o p n -> (o p) n")).then_inc(mask_in[t.slot(0)], 16)
                        if t.live(-1):
                            wait(sp, x1_ready, t.item(1) + 1)
                            sp.dma_start(x_s[t.slot(-1)][:, :],
                                         x[bass.ds(t.item(-1), 1), :, :].rearrange("o p n -> (o p) n")).then_inc(x_in[t.slot(-1)], 16)
                        if t.live(3):
                            sp.wait_ge(x2_ready, t.item(3) + 1)
                            sp.dma_start(x2_d[bass.ds(t.item(3) * P, P), :], x2[t.slot(3)][:, :]).then_inc(x2_out[t.slot(3)], 16)

                    pipeline(sp, iteration)
                    for p in (0, 1):
                        sp.wait_ge(x2_out[p], 16 * (NB // 2))

                @block.gpsimd
                def _(pool):
                    nc.gpsimd.memset(zeros[:, :], 0).then_inc(zeroed, 1)
                    nc.gpsimd.memset(ident[:, :], 0.0).then_inc(consts, 1)
                    nc.gpsimd.memset(ones_b[:, :], 1.0).then_inc(consts, 1)
                    nc.gpsimd.memset(causal_b[:, :], 0.0).then_inc(consts, 1)
                    nc.gpsimd.memset(before_b[:, :], 1.0).then_inc(consts, 1)
                    nc.gpsimd.memset(own_head[:, :], 1.0).then_inc(consts, 1)
                    nc.gpsimd.iota(token_no[:, :], pattern=[[P, NB]], base=0, channel_multiplier=1).then_inc(consts, 1)
                    nc.gpsimd.iota(iota_e[:, :], pattern=[[1, E]], base=0, channel_multiplier=0,
                                   allow_small_or_imprecise_dtypes=True).then_inc(consts, 1)
                    nc.gpsimd.iota(group_first[:, :], pattern=[[E, NGRP], [0, TOPK]], base=0, channel_multiplier=0,
                                   allow_small_or_imprecise_dtypes=True).then_inc(consts, 1)
                    for p in (0, 1):
                        nc.gpsimd.memset(kD[p][:, :, :], 0.0).then_inc(consts, 1)
                        nc.gpsimd.memset(xvD[p][:, :, :, :, :], 0.0).then_inc(consts, 1)
                    nc.gpsimd.memset(picked[:, :], 0.0).then_inc(consts, 1)
                    nc.gpsimd.memset(mv[:, :, :], 1.0).then_inc(consts, 1)
                    pool.wait_ge(consts, 14)
                    nc.gpsimd.affine_select(out=ident[:, :], in_=ident[:, :], compare_op=ALU.not_equal, fill=1.0,
                                            base=0, pattern=[[-1, P]], channel_multiplier=1).then_inc(consts, 1)
                    nc.gpsimd.affine_select(out=causal_b[:, :], in_=causal_b[:, :], compare_op=ALU.is_ge, fill=-BIG,
                                            base=0, pattern=[[-1, P]], channel_multiplier=1).then_inc(consts, 1)
                    nc.gpsimd.affine_select(out=before_b[:, :], in_=before_b[:, :], compare_op=ALU.is_gt, fill=0.0,
                                            base=0, pattern=[[1, P]], channel_multiplier=-1).then_inc(consts, 1)
                    nc.gpsimd.affine_select(out=own_head[:, :], in_=own_head[:, :], compare_op=ALU.is_ge, fill=0.0,
                                            base=0, pattern=[[-XD, XPC]], channel_multiplier=1).then_inc(consts, 1)
                    pool.wait_ge(consts, 18)
                    nc.gpsimd.affine_select(out=own_head[:, :], in_=own_head[:, :], compare_op=ALU.is_ge, fill=0.0,
                                            base=XD - 1, pattern=[[XD, XPC]], channel_multiplier=-1).then_inc(consts, 1)
                    nc.gpsimd.tensor_copy(ident_b[:, :], ident[:, :]).then_inc(consts, 1)
                    pool.wait_ge(weights_in, W_IN)
                    nc.gpsimd.partition_broadcast(xbv_s[:, :], bias_row[0:1, 0, :]).then_inc(consts, 1)
                    nc.gpsimd.partition_broadcast(xbo_s[:, :], bias_row[0:1, 1, :]).then_inc(consts, 1)
                    pool.wait_ge(consts, 22)
                    pool.wait_ge(list_clear, 16 * (NE * N // P // min(512, NE * N // P)))

                    def iteration(t):
                        if t.live(4):
                            pool.wait_ge(place_ready, t.item(4) + 1)
                            settle(pool, settled)
                            p = t.slot(4)
                            for j in range(SLOTS):
                                nc.gpsimd.indirect_dma_start(
                                    list_d[:, :], bass.IndirectOffsetOnAxis(ap=place[p][:, j:j + 1].bitcast(U32), axis=0),
                                    token[p][:, :], None).then_inc(placed[p], 16)
                        if t.live(1):
                            pool.wait_ge(x1_ready, t.item(1) + 1)
                            nc.gpsimd.tensor_tensor(x1b[t.slot(1)][:, :], x1[t.slot(1)][:, :], xbo_s[:, :], ALU.add).then_inc(x1b_ready, 1)

                    pipeline(pool, iteration)
                    for p in (0, 1):
                        pool.wait_ge(placed[p], 16 * SLOTS * (NB // 2))

                @block.tensor
                def _(pe):
                    pe.wait_ge(weights_in, W_IN)
                    pe.wait_ge(consts, 22)

                    def chunks(out_ap, lhs, rhs, n=KC):
                        for k in range(n):
                            last = nc.tensor.matmul(out_ap, lhs(k), rhs(k), start=(k == 0), stop=(k == n - 1))
                        return last

                    def job(t, n):
                        step, name, lag, col = JOBS[n]
                        if not t.live(lag):
                            return
                        for prior, count in bank_before(t, n):
                            wait(pe, moved[prior], count * MOVES.get(prior, 1))
                        o, p = JB[BANK[name]][:, col:], t.slot(lag)
                        if name in ("q0", "q1", "k0", "k1"):
                            w = wq_s if name[0] == "q" else wk_s
                            pe.wait_ge(xT_in[p], (t.turn(lag) + 1) * 16)
                            for c in range(4):
                                f = (4 * int(name[1]) + c) * P
                                last = chunks(o[:, c * P:(c + 1) * P], lambda k: w[:, k, f:f + P], lambda k: xT_s[p][:, k, :])
                        elif name in ("v0", "v1"):
                            f = 512 * int(name[1])
                            last = chunks(o[:, :], lambda k: xT_s[p][:, k, :], lambda k: wv_s[:, k, f:f + 512])
                        elif name == "o1":
                            pe.wait_ge(yT_in, (t.item(lag) + 1) * NG)
                            last = chunks(o[:, 0:D], lambda c: yT[:, c, :], lambda c: wo_s[:, c, :], PAIRS)
                        elif name == "o2":
                            pe.wait_ge(xyT_in, (t.item(lag) + 1) * NG)
                            last = chunks(o[:, 0:D], lambda c: xyT[:, c, :], lambda c: xwo_s[:, c, :])
                        elif name in ("x1t", "x2t"):
                            src, ready = (x1, x1_ready) if name == "x1t" else (x2, x2_ready)
                            pe.wait_ge(ready, t.item(lag) + 1)
                            for k in range(KC):
                                last = nc.tensor.transpose(o[:, k * P:(k + 1) * P], src[p][:, k * P:(k + 1) * P], ident[:, :])
                        elif name in ("xq", "xk"):
                            if name == "xq":
                                pe.wait_ge(moved["x1t"], t.item(lag) + 1)
                                w, r = xwq_s, x1T
                            else:
                                pe.wait_ge(cT_in[p], (t.turn(lag) + 1) * 16)
                                w, r = xwk_s, cT_s[p]
                            for m in range(KC):
                                last = chunks(o[:, m * P:(m + 1) * P], lambda k: w[:, k, m * P:(m + 1) * P], lambda k: r[:, k, :])
                        elif name == "route":
                            pe.wait_ge(moved["x2t"], t.item(lag) + 1)
                            last = chunks(o[:, 0:NE], lambda k: x2T[:, k, :], lambda k: router_s[:, k, :])
                        elif name == "rank":
                            pe.wait_ge(hot_ready, t.item(lag) + 1)
                            wait(pe, picked_ready, t.item(lag))
                            nc.tensor.matmul(o[:, 0:NE], before_b[:, :], hot_b[:, :, :].rearrange("p g e -> p (g e)"), start=True, stop=False)
                            last = nc.tensor.matmul(o[:, 0:NE], ones_b[:, :], picked[:, :], start=False, stop=True)
                        else:
                            last = chunks(o[:, 0:D], lambda k: cT_s[p][:, k, :], lambda k: xwv_s[:, k, :])
                        last.then_inc(made[name], 1)

                    def iteration(t):
                        for s in range(NG):
                            if t.live(0):
                                p = t.slot(0)
                                if s == 0:
                                    for n in ("q0", "q1", "k0", "k1"):
                                        pe.wait_ge(moved[n], (t.item(0) + 1) * MOVES.get(n, 1))
                                wait(pe, exped, t.item(0) * NG + s)
                                nc.tensor.matmul(S[:, :].rearrange("p (h k) -> p h k", h=GH), ident_b[:, :],
                                                 spread(causal_b[:, :], 1, GH), start=True, stop=False)
                                for j in range(GH // 2):
                                    c = s * GH // 2 + j
                                    last = nc.tensor.matmul(S[:, j * 2 * P:(j + 1) * 2 * P], qT[p][:, c, :], kD[p][:, c, :],
                                                            start=False, stop=(j == GH // 2 - 1))
                                last.then_inc(scores, 1)
                            if t.live(2):
                                p = t.slot(2)
                                if s == 0:
                                    pe.wait_ge(moved["xq"], t.item(2) + 1)
                                    pe.wait_ge(moved["xk"], t.item(2) + 1)
                                    pe.wait_ge(xmask_ready, t.item(2) + 1)
                                wait(pe, xexped, t.item(2) * NG + s)
                                nc.tensor.matmul(XS[:, :].rearrange("p (h k) -> p h k", h=GH), ident_b[:, :],
                                                 spread(xmask_b[p][:, :], 1, GH), start=True, stop=False)
                                c, j = divmod(s * GH, XPC)
                                nc.tensor.matmul(XS[:, :], xqT[p][:, c, :], xkD[p][:, c, j:j + GH, :].rearrange("p h k -> p (h k)"),
                                                 start=False, stop=True).then_inc(xscores, 1)
                            lag, g = behind(s, 0)
                            xlag, xg = behind(s, 2)
                            if t.live(lag):
                                pe.wait_ge(normed, t.item(lag) * NG + (g + 1))
                                wait(pe, probT_in, t.item(lag) * NG + g)
                                for h in range(GH):
                                    last = nc.tensor.transpose(T[:, h * P:(h + 1) * P], prob[g % 2][:, h, :], ident[:, :])
                                last.then_inc(turned, 1)
                            if t.live(xlag):
                                pe.wait_ge(xnormed, t.item(xlag) * NG + (xg + 1))
                                wait(pe, xprobT_in, t.item(xlag) * NG + xg)
                                for h in range(GH):
                                    last = nc.tensor.transpose(XT[:, h * P:(h + 1) * P], xprob[xg % 2][:, h, :], ident[:, :])
                                last.then_inc(xturned, 1)
                            for n, (step, *_) in enumerate(JOBS):
                                if step == s:
                                    job(t, n)
                            if t.live(lag):
                                pe.wait_ge(probT_in, t.item(lag) * NG + (g + 1))
                                wait(pe, yT_in, t.item(lag) * NG + g)
                            if t.live(xlag):
                                pe.wait_ge(xprobT_in, t.item(xlag) * NG + (xg + 1))
                                wait(pe, xyT_in, t.item(xlag) * NG + xg)
                            if t.live(lag):
                                if g == 0:
                                    pe.wait_ge(moved["v0"], t.item(lag) + 1)
                                    pe.wait_ge(moved["v1"], t.item(lag) + 1)
                                v = v_s[t.slot(lag)]
                                for h in range(GH):
                                    f = (g * GH + h) * DH
                                    r = DH * (h % 2)
                                    last = nc.tensor.matmul(PV[r:r + DH, (h // 2) * P:(h // 2 + 1) * P], v[:, f:f + DH], probT[:, h, :],
                                                            start=True, stop=True)
                                last.then_inc(mixed, 1)
                            if t.live(xlag):
                                if xg == 0:
                                    pe.wait_ge(moved["xv"], t.item(xlag) + 1)
                                for j in (0, 1):
                                    for quarter in range(GH // 2):
                                        c, n = divmod(xg * GH // 2 + quarter, QUARTERS)
                                        r = 2 * XD * n
                                        last = nc.tensor.matmul(PV[r:r + 2 * XD, CROSS], xvD[t.slot(xlag)][:, c, n, j, :], xprobT[:, 2 * quarter + j, :],
                                                                start=(j == 0), stop=(j == 1))
                                last.then_inc(xmixed, 1)

                    pipeline(pe, iteration)

                @block.scalar
                def _(act):
                    act.wait_ge(consts, 22)

                    def exponentials(bank, src_bias, dst, acc):
                        for h in range(GH):
                            last = nc.scalar.activation(dst[:, h, :], bank[:, h * P:(h + 1) * P], ACT.Exp,
                                                        bias=src_bias[:, h:h + 1], accum_out=acc[:, h:h + 1])
                        return last

                    def iteration(t):
                        for s in range(NG):
                            lag, g = behind(s, 0)
                            xlag, xg = behind(s, 2)
                            if t.live(0):
                                act.wait_ge(maxed, t.item(0) * NG + (s + 1))
                                exponentials(S, negmax[s % 2], prob[s % 2], total[s % 2]).then_inc(exped, 1)
                            if t.live(lag):
                                act.wait_ge(turned, t.item(lag) * NG + (g + 1))
                                nc.scalar.copy(probT[:, :, :].rearrange("p h q -> p (h q)"), T[:, :]).then_inc(probT_in, 1)
                            if t.live(xlag):
                                act.wait_ge(xturned, t.item(xlag) * NG + (xg + 1))
                                nc.scalar.copy(xprobT[:, :, :].rearrange("p h q -> p (h q)"), XT[:, :]).then_inc(xprobT_in, 1)
                            if t.live(2):
                                act.wait_ge(xmaxed, t.item(2) * NG + (s + 1))
                                exponentials(XS, xnegmax[s % 2], xprob[s % 2], xtotal[s % 2]).then_inc(xexped, 1)
                            if s == 2:
                                if t.live(-1):
                                    for n in (0, 1):
                                        act.wait_ge(made[f"k{n}"], t.item(-1) + 1)
                                        nc.scalar.copy(kD[t.slot(-1)][0:DH, 4 * n:4 * n + 4, 0:P],
                                                       JB[BANK[f"k{n}"]][0:DH, :].rearrange("p (c k) -> p c k", c=4)).then_inc(moved[f"k{n}"], 1)
                                joined = [(n, lg) for n, lg in (("x1t", 1), ("x2t", 3)) if t.live(lg)]
                                for n, lg in joined:
                                    act.wait_ge(made[n], t.item(lg) + 1)
                                for n, lg in joined:
                                    dst, c = (x1T, 0) if n == "x1t" else (x2T, D)
                                    nc.scalar.copy(dst[:, :, :].rearrange("p k t -> p (k t)"), JB[BANK[n]][:, c:c + D]).then_inc(moved[n], 1)
                            if s == 3:
                                if t.live(-1):
                                    act.wait_ge(made["v0"], t.item(-1) + 1)
                                    nc.scalar.copy(v_s[t.slot(-1)][:, 0:512], JB[BANK["v0"]][:, :]).then_inc(moved["v0"], 1)
                                if t.live(3):
                                    act.wait_ge(moved["route"], t.item(3) + 1)
                                    nc.scalar.activation(soft[:, :], below[:, :], ACT.Exp).then_inc(soft_ready, 1)
                                if t.live(-1):
                                    act.wait_ge(made["v1"], t.item(-1) + 1)
                                    nc.scalar.copy(v_s[t.slot(-1)][:, 512:1024], JB[BANK["v1"]][:, :]).then_inc(moved["v1"], 1)
                            if t.live(lag):
                                act.wait_ge(mixed, t.item(lag) * NG + (g + 1))
                            if t.live(xlag):
                                act.wait_ge(xmixed, t.item(xlag) * NG + (xg + 1))
                            if t.live(lag):
                                nc.scalar.copy(yT[:, 2 * g:2 * g + 2, :].rearrange("p c q -> p (c q)"), PV[:, SELF]).then_inc(yT_in, 1)
                            if t.live(xlag):
                                half = slice(xg % 2 * P // 2, (xg % 2 + 1) * P // 2)
                                nc.scalar.copy(xyT[half, xg // 2, :], PV[half, CROSS]).then_inc(xyT_in, 1)

                    pipeline(act, iteration)

                @block.vector
                def _(dve):
                    dve.wait_ge(consts, 22)

                    def negated_max(dst, bank):
                        return nc.vector.tensor_reduce(dst[:, :], bank[:, :].rearrange("p (h k) -> p h k", h=GH), AX.X, ALU.max, negate=True)

                    def normalise(t, s):
                        if t.live(0):
                            dve.wait_ge(exped, t.item(0) * NG + (s + 1))
                            nc.vector.reciprocal(inv[:, :], total[s % 2][:, :]).then_inc(inv_ready, 1)
                        if t.live(2):
                            dve.wait_ge(xexped, t.item(2) * NG + (s + 1))
                            nc.vector.reciprocal(xinv[:, :], xtotal[s % 2][:, :]).then_inc(xinv_ready, 1)
                        if t.live(0):
                            dve.wait_ge(inv_ready, t.item(0) * NG + (s + 1))
                            nc.vector.tensor_tensor(prob[s % 2][:, :, :], prob[s % 2][:, :, :], spread(inv[:, :], 2, P), ALU.mult).then_inc(normed, 1)
                        if t.live(2):
                            dve.wait_ge(xinv_ready, t.item(2) * NG + (s + 1))
                            nc.vector.tensor_tensor(xprob[s % 2][:, :, :], xprob[s % 2][:, :, :], spread(xinv[:, :], 2, P), ALU.mult).then_inc(xnormed, 1)

                    def norms_begin(t):
                        two_, one_, four = t.live(3), t.live(1), t.live(4)
                        if two_:
                            dve.wait_ge(made["o2"], t.item(3) + 1)
                        if four:
                            dve.wait_ge(made["rank"], t.item(4) + 1)
                        if two_:
                            steps2 = Steps(dve, norm2_step, 2, t.item(3))
                            dve.wait_ge(x1b_ready, t.item(3) + 1)
                            nc.vector.tensor_tensor(sum2[:, :], JB[BANK["o2"]][:, 0:D], x1b[t.slot(3)][:, :], ALU.add).then_inc(moved["o2"], 1)
                        if four:
                            nc.vector.tensor_tensor(hot_rank[:, :, :, :], hot[:, :, :, :],
                                                    spread(JB[BANK["rank"]][:, D:D + NE].rearrange("p (g e) -> p g e", g=NGRP), 2, TOPK),
                                                    ALU.mult).then_inc(moved["rank"], 1)
                        if two_:
                            dve.wait_ge(moved["o2"], t.item(3) + 1)
                            steps2.done(nc.vector.bn_stats(stats[:, 1, :], sum2[:, :]))
                        if one_:
                            steps1 = Steps(dve, norm1_step, 2, t.item(1))
                            dve.wait_ge(made["o1"], t.item(1) + 1)
                            dve.wait_ge(x_in[t.slot(1)], (t.turn(1) + 1) * 16)
                            nc.vector.tensor_tensor(sum1[:, :], JB[BANK["o1"]][:, 0:D], x_s[t.slot(1)][:, :], ALU.add).then_inc(moved["o1"], 1)
                        if two_:
                            steps2.need()
                            settle(dve, settled)
                            steps2.done(nc.vector.bn_aggr(mv[:, 1, :], stats[:, 1, :]))
                        if one_:
                            dve.wait_ge(moved["o1"], t.item(1) + 1)
                            steps1.done(nc.vector.bn_stats(stats[:, 0, :], sum1[:, :]))
                            steps1.need()
                            settle(dve, settled)
                            steps1.done(nc.vector.bn_aggr(mv[:, 0, :], stats[:, 0, :]))
                        if one_ or two_:
                            if two_:
                                steps2.need()
                            if one_:
                                steps1.need()
                            steps = Steps(dve, rsqrt_step, RSQRT_STEPS, t.item(1))
                            rsqrt_begin(steps, (mv[:, :, 1], *(rs[:, :, c] for c in range(5))))
                            return steps

                    def norms_end(t, steps):
                        two_, one_ = t.live(3), t.live(1)
                        if one_ or two_:
                            rsqrt_end(steps, (mv[:, :, 1], *(rs[:, :, c] for c in range(5))))
                            steps.need()
                        if two_:
                            wait(dve, x2_out[t.slot(3)], t.turn(3) * 16)
                            nc.vector.tensor_scalar(x2[t.slot(3)][:, :], sum2[:, :], mv[:, 1, 0:1], rs[:, 1, 2:3],
                                                    ALU.subtract, ALU.mult).then_inc(x2_ready, 1)
                        if one_:
                            nc.vector.tensor_scalar(x1[t.slot(1)][:, :], sum1[:, :], mv[:, 0, 0:1], rs[:, 0, 2:3],
                                                    ALU.subtract, ALU.mult).then_inc(x1_ready, 1)

                    def place_tokens(t):
                        if not t.live(4):
                            return
                        b, p = t.item(4), t.slot(4)
                        steps = Steps(dve, place_step, 1, b)
                        rank_b = rank[:, bass.ds(b, 1), :].rearrange("p o s -> p (o s)")
                        nc.vector.tensor_tensor(picked[:, :], picked[:, :], hot_b[:, :, :].rearrange("p g e -> p (g e)"), ALU.add).then_inc(picked_ready, 1)
                        dve.wait_ge(moved["rank"], b + 1)
                        steps.done(nc.vector.tensor_reduce(rank_b, hot_rank[:, :, :, :].rearrange("p g k e -> p (g k) e"), AX.X, ALU.add))
                        wait(dve, placed[p], t.turn(4) * 16 * SLOTS)
                        nc.vector.tensor_copy(token[p][:, :], token_no[:, bass.ds(b, 1)])
                        steps.need()
                        dve.wait_ge(list_row_ready, b + 1)
                        nc.vector.tensor_tensor(place[p][:, :], list_row[:, :], rank_b, ALU.add).then_inc(place_ready, 1)

                    def top_two(t):
                        if not t.live(3):
                            return
                        steps = Steps(dve, route_step, 6, t.item(3))
                        dve.wait_ge(made["route"], t.item(3) + 1)
                        settle(dve, settled)
                        lg = JB[BANK["route"]][:, D:D + NE].rearrange("p (g e) -> p g e", g=NGRP)
                        for g in range(NGRP):
                            steps.done(nc.vector.max(top8[:, g, :], lg[:, g, :]))
                        steps.need()
                        settle(dve, settled)
                        for g in range(NGRP):
                            steps.done(nc.vector.max_index(top8i[:, g, :], top8[:, g, :], lg[:, g, :]))
                        steps.done(nc.vector.tensor_tensor(below[:, NE:NE + NGRP], top8[:, :, 1], top8[:, :, 0], ALU.subtract))
                        nc.vector.tensor_tensor(below[:, 0:NE].rearrange("p (g e) -> p g e", g=NGRP), lg,
                                                top8[:, :, 0:1].broadcast_to([P, NGRP, E]), ALU.subtract).then_inc(moved["route"], 1)
                        steps.need(4)
                        steps.done(nc.vector.tensor_copy(choice[:, :, :], top8i[:, :, 0:TOPK]))

                    def weigh(t):
                        if not t.live(3):
                            return
                        b = t.item(3)
                        steps = Steps(dve, weigh_step, 4, b)
                        of_batch = expert[:, bass.ds(b, 1), :].rearrange("p o s -> p (o s)")
                        w_batch = weight[:, bass.ds(b, 1), :].rearrange("p o (g k) -> p (o g) k", g=NGRP)
                        dve.wait_ge(route_step, b * 6 + 6)
                        steps.done(nc.vector.tensor_tensor(hot[:, :, :, :].rearrange("p g k e -> p (g k) e"), spread(iota_e[:, :], 1, SLOTS),
                                                           spread(choice[:, :, :].rearrange("p g k -> p (g k)"), 2, E), ALU.is_equal))
                        dve.wait_ge(soft_ready, b + 1)
                        steps.done(nc.vector.tensor_reduce(soft_sum[:, :], soft[:, 0:NE].rearrange("p (g e) -> p g e", g=NGRP), AX.X, ALU.add))
                        steps.done(nc.vector.tensor_tensor(of_batch, choice[:, :, :].rearrange("p g k -> p (g k)"), group_first[:, :], ALU.add))
                        steps.need(1)
                        nc.vector.tensor_tensor(hot_b[:, :, :], hot[:, :, 0, :], hot[:, :, 1, :], ALU.add).then_inc(hot_ready, 1)
                        steps.need(2)
                        steps.done(nc.vector.reciprocal(soft_inv[:, :], soft_sum[:, :]))
                        steps.need(3)
                        nc.vector.tensor_scalar(list_row[:, :], of_batch, float(N), None, ALU.mult).then_inc(list_row_ready, 1)
                        steps.need(4)
                        nc.vector.tensor_scalar(w_batch[:, :, 0], soft_inv[:, :], 1.0 / NGRP, None, ALU.mult)
                        nc.vector.scalar_tensor_tensor(w_batch[:, :, 1], soft[:, NE:NE + NGRP], 1.0 / NGRP, soft_inv[:, :], ALU.mult, ALU.mult)

                    def iteration(t):
                        for s in range(NG):
                            if t.live(0):
                                dve.wait_ge(scores, t.item(0) * NG + (s + 1))
                                negated_max(negmax[s % 2], S).then_inc(maxed, 1)
                            if t.live(2):
                                dve.wait_ge(xscores, t.item(2) * NG + (s + 1))
                                negated_max(xnegmax[s % 2], XS).then_inc(xmaxed, 1)
                            if s == 0:
                                if t.live(-1):
                                    for n in (0, 1):
                                        dve.wait_ge(made[f"q{n}"], t.item(-1) + 1)
                                        nc.vector.tensor_scalar(qT[t.slot(-1)][:, 4 * n:4 * n + 4, :].rearrange("p c q -> p (c q)"),
                                                                JB[BANK[f"q{n}"]][:, :], DH ** -0.5, None, ALU.mult).then_inc(moved[f"q{n}"], 1)
                                normalise(t, s)
                            if s == 1:
                                normalise(t, s)
                                norm_steps = norms_begin(t)
                                place_tokens(t)
                            if s == 2:
                                norms_end(t, norm_steps)
                                if t.live(-1):
                                    for n in (0, 1):
                                        dve.wait_ge(made[f"k{n}"], t.item(-1) + 1)
                                        nc.vector.tensor_copy(kD[t.slot(-1)][DH:P, 4 * n:4 * n + 4, P:2 * P],
                                                              JB[BANK[f"k{n}"]][DH:P, :].rearrange("p (c k) -> p c k", c=4)).then_inc(moved[f"k{n}"], 1)
                                normalise(t, s)
                                if t.live(1):
                                    dve.wait_ge(made["xk"], t.item(1) + 1)
                                    for m in range(KC):
                                        last = nc.vector.scalar_tensor_tensor(
                                            xkD[t.slot(1)][:, m, :, :], spread(JB[BANK["xk"]][:, m * P:(m + 1) * P], 1, XPC), xbk_s[:, m:m + 1],
                                            spread(own_head[:, :], 2, P), ALU.add, ALU.mult)
                                    last.then_inc(moved["xk"], 1)
                            if s == 3:
                                if t.live(3):
                                    dve.wait_ge(made["route"], t.item(3) + 1)
                                if t.live(1):
                                    dve.wait_ge(made["xq"], t.item(1) + 1)
                                    for m in range(KC):
                                        last = nc.vector.tensor_scalar(xqT[t.slot(1)][:, m, :], JB[BANK["xq"]][:, m * P:(m + 1) * P], xbq_s[:, m:m + 1],
                                                                       XD ** -0.5, ALU.add, ALU.mult)
                                    last.then_inc(moved["xq"], 1)
                                top_two(t)
                                normalise(t, s)
                                if t.live(1):
                                    dve.wait_ge(made["xv"], t.item(1) + 1)
                                    for m in range(KC):
                                        for j in (0, 1):
                                            last = nc.vector.tensor_tensor(
                                                xvD[t.slot(1)][:, m, :, j, j * XD:(j + 1) * XD],
                                                JB[BANK["xv"]][:, m * P:(m + 1) * P].rearrange("p (h j d) -> p h j d", h=QUARTERS, j=2)[:, :, j, :],
                                                xbv_s[:, m * P:(m + 1) * P].rearrange("p (h j d) -> p h j d", h=QUARTERS, j=2)[:, :, j, :], ALU.add)
                                    last.then_inc(moved["xv"], 1)
                                if t.live(1):
                                    dve.wait_ge(mask_in[t.slot(1)], (t.turn(1) + 1) * 16)
                                    nc.vector.tensor_scalar(xmask_b[t.slot(1)][:, :], mask_s[t.slot(1)][:, :], 0.0, -BIG,
                                                            ALU.is_equal, ALU.mult).then_inc(xmask_ready, 1)
                                weigh(t)

                    pipeline(dve, iteration)

        with ExitStack() as two:
            def sb(name, shape, dt=F32):
                return tile(two, name, shape, dt)

            moe = sb("moe", [P, 3 * HALF, WCOL])
            moe_cols = moe[:, :, :].rearrange("p e n -> p (e n)")
            thirds = [moe[:, n * HALF:(n + 1) * HALF, :] for n in range(3)]

            tile_no = sb("tile_no", [P, NGRP, TA])
            late = sb("late", [P, TA])
            counts_i = [sb(f"counts_i{i}", [P, NE], I32) for i in (0, 1)]
            ntiles = sb("ntiles", [P, NGRP, E])
            ends = [sb(f"ends{i}", [P, NGRP, E]) for i in (0, 1)]
            first_row = sb("first_row", [P, NE])
            passed = sb("passed", [P, NGRP, TA, E])
            passed_n = sb("passed_n", [P, NGRP, TA, E])
            tile_e, tile_j, tile_l = (sb(n, [P, NGRP, TA]) for n in ("tile_e", "tile_j", "tile_l"))
            tile_w, tile_wrap = sb("tile_w", [P, TA]), sb("tile_wrap", [P, TA])
            mix = [sb(f"mix{i}", [P, TA]) for i in range(3)]
            list_no, weight_col = sb("list_no", [P, TA], I32), sb("weight_col", [P, TA], I32)
            weight_tab = sb("weight_tab", [1, TA * P], I32)
            lists = sb("lists", [P, TA, P], I32)
            lists_f = sb("lists_f", [P, TA, P])
            tokens = sb("tokens", [P, TA * P], I32)
            row = sb("row", [P, NB * SLOTS])
            match = [sb(f"match{i}", [P, NB * SLOTS]) for i in (0, 1)]
            NQ = 4
            who = [sb(f"who{q}", [P, 1], I32) for q in range(NQ)]
            xg_s = [sb(f"xg{q}", [P, D]) for q in range(NQ)]
            xgT = [sb(f"xgT{q}", [P, KC, P]) for q in (0, 1)]
            gate_s = [sb(f"gate{q}", [P, HID]) for q in (0, 1)]
            h_s = [sb(f"h{q}", [P, HID]) for q in (0, 1)]
            hT_s = [sb(f"hT{q}", [P, P]) for q in (0, 1)]
            y_s = [sb(f"y{q}", [P, D]) for q in range(NQ)]
            XB, GB, HB, YB = banks[0:2], banks[2:4], banks[4], banks[5:7]

            link, counted, tab_out, tab_in, lists_in, lists_fp, lists_t, tokens_ready = (
                sem(n) for n in ("link", "counted", "tab_out", "tab_in", "lists_in", "lists_fp", "lists_t", "tokens_ready"))
            moe_in = [sem(f"moe_in{n}") for n in range(4)]
            iotas, tabs_ready = sem("iotas"), sem("tabs_ready")
            who_ready = sem("who_ready")
            xg_in = [sem(f"xg_in{q}") for q in range(NQ)]
            xgt_made, xgt_in, gu_made, gate_in, h_in, ht_made, ht_in, y_made, y_in = (
                sem(n) for n in ("xgt_made", "xgt_in", "gu_made", "gate_in", "h_in", "ht_made", "ht_in", "y_made", "y_in"))
            y_out = [sem(f"y_out{q}") for q in range(NQ)]

            def group_tiles(eng, g, iteration):
                lo, hi = g * TILES, (g + 1) * TILES
                for n in range(lo, lo + 2 * NQ):
                    iteration(at(n, NQ, lo, hi))
                with eng.Fori(lo // NQ + 2, hi // NQ - 1) as u:
                    for q in range(NQ):
                        iteration(When(u, q, NQ, lo, hi))
                for n in range(hi - NQ, hi + NQ):
                    iteration(at(n, NQ, lo, hi))

            with nc.Block() as block:
                @block.sync
                def _(sp):
                    load_experts(sp, thirds[0], 0, g0, u0, d0, moe_in[0])
                    load_experts(sp, thirds[1], HALF, g0, u0, d0, moe_in[1])
                    sp.wait_ge(tabs_ready, 1)
                    sp.dma_start(tab_d.rearrange("(p a) -> p a", p=P), weight_col[:, :]).then_inc(tab_out, 16)
                    sp.wait_ge(tab_out, 16)
                    sp.dma_start(weight_tab[0:1, :], tab_d.rearrange("(o n) -> o n", o=1)).then_inc(tab_in, 16)
                    load_experts(sp, thirds[2], 0, g1, u1, d1, moe_in[2])

                    def iteration(t):
                        if t.live(3):
                            sp.wait_ge(y_in, t.item(3) + 1)
                            sp.dma_start(y_d[bass.ds(t.item(3) * P, P), :], y_s[t.slot(3)][:, :]).then_inc(y_out[t.slot(3)], 16)

                    group_tiles(sp, 0, iteration)
                    sp.wait_ge(y_made, TILES)
                    load_experts(sp, thirds[0], HALF, g1, u1, d1, moe_in[3])
                    group_tiles(sp, 1, iteration)
                    for q in range(NQ):
                        sp.wait_ge(y_out[q], 16 * (NT // NQ))

                @block.gpsimd
                def _(pool):
                    nc.gpsimd.iota(tile_no[:, :, :], pattern=[[-TILES, NGRP], [1, TA]], base=0, channel_multiplier=TA,
                                   allow_small_or_imprecise_dtypes=True).then_inc(iotas, 1)
                    pool.wait_ge(tabs_ready, 1)
                    for a in range(TA):
                        nc.gpsimd.indirect_dma_start(
                            lists[:, a, :], None, list_d.rearrange("(r n) o -> r (n o)", n=P),
                            bass.IndirectOffsetOnAxis(ap=list_no[:, a:a + 1].bitcast(U32), axis=0)).then_inc(lists_in, 16)

                    def iteration(t):
                        if t.live(0):
                            q = t.slot(0)
                            pool.wait_ge(who_ready, t.item(0) + 1)
                            wait(pool, xgt_made, t.item(NQ) + 1)
                            settle(pool, settled)
                            nc.gpsimd.indirect_dma_start(
                                xg_s[q][:, :], None, x2_d[:, :],
                                bass.IndirectOffsetOnAxis(ap=who[q][:, :].bitcast(U32), axis=0)).then_inc(xg_in[q], 16)

                    for g in range(NGRP):
                        group_tiles(pool, g, iteration)

                @block.tensor
                def _(pe):
                    nc.tensor.matmul(banks[7][:, 0:NE], ones_b[:, :], picked[:, :], start=True, stop=True).then_inc(counted, 1)
                    pe.wait_ge(lists_fp, 1)
                    for a in range(TA):
                        last = nc.tensor.transpose(banks[a // 4][:, (a % 4) * P:(a % 4 + 1) * P], lists_f[:, a, :], ident[:, :])
                    last.then_inc(lists_t, 1)
                    pe.wait_ge(tokens_ready, 1)
                    pe.wait_ge(tab_in, 16)

                    def weights(t, lag):
                        return pe.value_load(weight_tab[0:1, bass.ds(t.item(lag), 1)], min_val=0, max_val=(3 * HALF - 1) * WCOL)

                    def iteration(t):
                        if t.live(0):
                            q = t.slot(0)
                            pe.wait_ge(xg_in[q], (t.turn(0) + 1) * 16)
                            wait(pe, xgt_in, t.item(1))
                            for k in range(KC):
                                last = nc.tensor.transpose(XB[q % 2][:, k * P:(k + 1) * P], xg_s[q][:, k * P:(k + 1) * P], ident[:, :])
                            last.then_inc(xgt_made, 1)
                        if t.live(1):
                            q = t.slot(1)
                            first = weights(t, 1)
                            pe.wait_ge(xgt_in, t.item(1) + 1)
                            wait(pe, h_in, t.item(2))
                            for k in range(KC):
                                last = nc.tensor.matmul(GB[q % 2][:, 0:2 * HID], xgT[q % 2][:, k, :],
                                                        moe_cols[:, bass.ds(first + k * 2 * HID, 2 * HID)], start=(k == 0), stop=(k == KC - 1))
                            last.then_inc(gu_made, 1)
                        if t.live(2):
                            q = t.slot(2)
                            pe.wait_ge(h_in, t.item(2) + 1)
                            wait(pe, ht_in, t.item(2))
                            nc.tensor.transpose(HB[:, 0:P], h_s[q % 2][:, :], ident[:, :]).then_inc(ht_made, 1)
                        if t.live(3):
                            q = t.slot(3)
                            first = weights(t, 3)
                            pe.wait_ge(ht_in, t.item(3) + 1)
                            wait(pe, y_in, t.item(4))
                            nc.tensor.matmul(YB[q % 2][:, 0:D], hT_s[q % 2][:, :], moe_cols[:, bass.ds(first + KC * 2 * HID, D)],
                                             start=True, stop=True).then_inc(y_made, 1)

                    pe.wait_ge(moe_in[0], MOE_LOAD)
                    pe.wait_ge(moe_in[1], MOE_LOAD)
                    group_tiles(pe, 0, iteration)
                    pe.wait_ge(moe_in[2], MOE_LOAD)
                    pe.wait_ge(moe_in[3], MOE_LOAD)
                    group_tiles(pe, 1, iteration)

                @block.scalar
                def _(act):
                    def iteration(t):
                        if t.live(0):
                            q = t.slot(0)
                            act.wait_ge(xgt_made, t.item(0) + 1)
                            wait(act, gu_made, t.item(1))
                            nc.scalar.copy(xgT[q % 2][:, :, :].rearrange("p k t -> p (k t)"), XB[q % 2][:, 0:D]).then_inc(xgt_in, 1)
                        if t.live(1):
                            q = t.slot(1)
                            act.wait_ge(gu_made, t.item(1) + 1)
                            nc.scalar.activation(gate_s[q % 2][:, :], GB[q % 2][:, 0:HID], ACT.Silu).then_inc(gate_in, 1)
                        if t.live(2):
                            q = t.slot(2)
                            act.wait_ge(ht_made, t.item(2) + 1)
                            nc.scalar.copy(hT_s[q % 2][:, :], HB[:, 0:P]).then_inc(ht_in, 1)

                    for g in range(NGRP):
                        group_tiles(act, g, iteration)

                @block.vector
                def _(dve):
                    made = [0]

                    def linked(instruction):
                        made[0] += 1
                        instruction.then_inc(link, 1)
                        dve.wait_ge(link, made[0])

                    v = nc.vector
                    dve.wait_ge(counted, 1)
                    dve.wait_ge(iotas, 1)
                    linked(v.tensor_scalar(counts_i[0][:, :], banks[7][:, 0:NE], float(P - 1), None, ALU.add))
                    linked(v.tensor_single_scalar(counts_i[1][:, :], counts_i[0][:, :], P.bit_length() - 1, op=ALU.arith_shift_right))
                    linked(v.tensor_copy(ntiles[:, :, :].rearrange("p g e -> p (g e)"), counts_i[1][:, :]))
                    linked(v.tensor_copy(ends[0][:, :, :], ntiles[:, :, :]))
                    d, n = 1, 0
                    while d < E:
                        linked(v.tensor_copy(ends[1 - n][:, :, 0:d], ends[n][:, :, 0:d]))
                        linked(v.tensor_tensor(ends[1 - n][:, :, d:E], ends[n][:, :, d:E], ends[n][:, :, 0:E - d], ALU.add))
                        d, n = 2 * d, 1 - n
                    end = ends[n]
                    for g in range(NGRP):
                        linked(v.tensor_tensor(first_row[:, g * E:(g + 1) * E], end[:, g, :], ntiles[:, g, :], ALU.subtract))
                        linked(v.tensor_scalar(first_row[:, g * E:(g + 1) * E], first_row[:, g * E:(g + 1) * E], float(g * TILES), float(P),
                                               ALU.add, ALU.mult))
                    for g in range(NGRP):
                        linked(v.tensor_tensor(passed[:, g, :, :], spread(end[:, g, :], 1, TA), spread(tile_no[:, g, :], 2, E), ALU.is_le))
                        linked(v.tensor_tensor(passed_n[:, g, :, :], passed[:, g, :, :], spread(ntiles[:, g, :], 1, TA), ALU.mult))
                        linked(v.tensor_reduce(tile_e[:, g, :], passed[:, g, :, :], AX.X, ALU.add))
                        linked(v.tensor_reduce(tile_j[:, g, :], passed_n[:, g, :, :], AX.X, ALU.add))
                    linked(v.tensor_tensor(tile_j[:, :, :], tile_no[:, :, :], tile_j[:, :, :], ALU.subtract))
                    linked(v.tensor_scalar(tile_j[:, :, :], tile_j[:, :, :], float(N // P - 1), 0.0, ALU.min, ALU.max))
                    linked(v.tensor_scalar(tile_e[:, :, :], tile_e[:, :, :], float(E - 1), None, ALU.min))
                    linked(v.scalar_tensor_tensor(tile_l[:, :, :], tile_e[:, :, :], float(N // P), tile_j[:, :, :], ALU.mult, ALU.add))
                    linked(v.tensor_scalar(late[:, :], tile_no[:, 0, :], float(TILES), None, ALU.is_ge))
                    linked(v.tensor_scalar(mix[0][:, :], tile_l[:, 1, :], float(E * N // P), None, ALU.add))
                    linked(v.tensor_tensor(mix[1][:, :], mix[0][:, :], tile_l[:, 0, :], ALU.subtract))
                    linked(v.tensor_tensor(mix[2][:, :], mix[1][:, :], late[:, :], ALU.mult))
                    linked(v.tensor_tensor(list_no[:, :], mix[2][:, :], tile_l[:, 0, :], ALU.add))
                    linked(v.tensor_scalar(tile_wrap[:, :], tile_e[:, 1, :], float(HALF), -float(E + HALF), ALU.is_ge, ALU.mult))
                    linked(v.scalar_tensor_tensor(mix[0][:, :], tile_e[:, 1, :], float(E), tile_wrap[:, :], ALU.add, ALU.add))
                    linked(v.tensor_tensor(mix[1][:, :], mix[0][:, :], tile_e[:, 0, :], ALU.subtract))
                    linked(v.tensor_tensor(mix[2][:, :], mix[1][:, :], late[:, :], ALU.mult))
                    linked(v.tensor_tensor(tile_w[:, :], mix[2][:, :], tile_e[:, 0, :], ALU.add))
                    v.tensor_scalar(weight_col[:, :], tile_w[:, :], float(WCOL), None, ALU.mult).then_inc(tabs_ready, 1)
                    dve.wait_ge(lists_in, 16 * TA)
                    v.tensor_copy(lists_f[:, :, :], lists[:, :, :]).then_inc(lists_fp, 1)
                    dve.wait_ge(lists_t, 1)
                    for a in range(TA):
                        last = v.tensor_copy(tokens[:, :].rearrange("n (p a) -> n p a", a=TA)[:, :, a], banks[a // 4][:, (a % 4) * P:(a % 4 + 1) * P])
                    last.then_inc(tokens_ready, 1)
                    dve.wait_ge(tokens_ready, 1)

                    AHEAD = 2

                    def name_tokens(t, lag):
                        if t.live(lag):
                            q = t.slot(lag)
                            wait(dve, xg_in[q], t.turn(lag) * 16)
                            v.tensor_copy(who[q][:, :], tokens[:, bass.ds(t.item(lag), 1)]).then_inc(who_ready, 1)

                    def iteration(t):
                        name_tokens(t, -AHEAD)
                        if t.live(1):
                            q = t.slot(1)
                            dve.wait_ge(gate_in, t.item(1) + 1)
                            wait(dve, ht_made, t.item(2))
                            v.tensor_tensor(h_s[q % 2][:, :], gate_s[q % 2][:, :], GB[q % 2][:, HID:2 * HID], ALU.mult).then_inc(h_in, 1)
                        if t.live(3):
                            q = t.slot(3)
                            dve.wait_ge(y_made, t.item(3) + 1)
                            wait(dve, y_out[q], t.turn(3) * 16)
                            v.tensor_copy(y_s[q][:, :], YB[q % 2][:, 0:D]).then_inc(y_in, 1)

                    for g in range(NGRP):
                        for n in range(AHEAD):
                            name_tokens(at(g * TILES + n, NQ, g * TILES, (g + 1) * TILES), 0)
                        group_tiles(dve, g, iteration)
                        if g == 0:
                            linked(v.tensor_copy(row[:, :], rank[:, :, :].rearrange("p b s -> p (b s)")))
                            for e in range(NE):
                                linked(v.tensor_scalar(match[e % 2][:, :], expert[:, :, :].rearrange("p b s -> p (b s)"), float(e),
                                                       first_row[:, e:e + 1], ALU.is_equal, ALU.mult))
                                linked(v.tensor_tensor(row[:, :], row[:, :], match[e % 2][:, :], ALU.add))
                            linked(v.tensor_copy(row_i[:, :, :].rearrange("p b s -> p (b s)"), row[:, :]))

        with ExitStack() as three:
            def sb(name, shape, dt=F32):
                return tile(three, name, shape, dt)

            QUAD = 4
            QUADS = NB // QUAD
            halves = [(h, q) for h in (0, 1) for q in range(QUAD)]
            want = {k: sb(f"want{k[0]}{k[1]}", [P, SLOTS], I32) for k in halves}
            rows4 = {k: sb(f"rows{k[0]}{k[1]}", [P, SLOTS, D]) for k in halves}
            x2r = {k: sb(f"x2r{k[0]}{k[1]}", [P, D]) for k in halves}
            acc = [sb(f"acc{q}", [P, D]) for q in range(QUAD)]
            o_s = {k: sb(f"o{k[0]}{k[1]}", [P, D]) for k in halves}
            st4, mv4 = sb("st4", [P, QUAD, 6]), sb("mv4", [P, QUAD, 2])
            ve, bits, rstd, ya, yb = (sb(n, [P, QUAD]) for n in ("ve", "bits", "rstd", "ya", "yb"))
            rows_in = {k: sem(f"rows_in{k[0]}{k[1]}") for k in halves}
            x2r_in = {k: sem(f"x2r_in{k[0]}{k[1]}") for k in halves}
            out_done = {k: sem(f"out_done{k[0]}{k[1]}") for k in halves}
            want_ready, rows_used, o_ready, step_done = (sem(n) for n in ("want_ready", "rows_used", "o_ready", "step_done"))

            def quads(eng, body):
                for h in (0, 1):
                    body(h, h, 0)
                with eng.Fori(1, QUADS // 2 - 1) as u:
                    for h in (0, 1):
                        body(u * 2 + h, h, u)
                for h in (0, 1):
                    body(QUADS - 2 + h, h, QUADS // 2 - 1)

            with nc.Block() as block:
                @block.sync
                def _(sp):
                    def body(n, h, u):
                        for q in range(QUAD):
                            wait(sp, rows_used, (n - 2) * QUAD + (q + 1))
                            sp.dma_start(x2r[h, q][:, :], x2_d[bass.ds((n * QUAD + q) * P, P), :]).then_inc(x2r_in[h, q], 16)

                    quads(sp, body)

                @block.gpsimd
                def _(pool):
                    def body(n, h, u):
                        for q in range(QUAD):
                            pool.wait_ge(want_ready, n * QUAD + (q + 1))
                            wait(pool, rows_used, (n - 2) * QUAD + (q + 1))
                            settle(pool, settled)
                            for j in range(SLOTS):
                                nc.gpsimd.indirect_dma_start(
                                    rows4[h, q][:, j, :], None, y_d[:, :],
                                    bass.IndirectOffsetOnAxis(ap=want[h, q][:, j:j + 1].bitcast(U32), axis=0)).then_inc(rows_in[h, q], 16)

                    quads(pool, body)

                @block.scalar
                def _(act):
                    def body(n, h, u):
                        for q in range(QUAD):
                            act.wait_ge(o_ready, n * QUAD + (q + 1))
                            act.dma_start(out[bass.ds(n * QUAD + q, 1), :, :].rearrange("o p d -> (o p) d"), o_s[h, q][:, :]).then_inc(out_done[h, q], 16)

                    quads(act, body)
                    for k in halves:
                        act.wait_ge(out_done[k], 16 * (QUADS // 2))

                @block.vector
                def _(dve):
                    v = nc.vector

                    def name_rows(n, h, u):
                        for q in range(QUAD):
                            wait(dve, rows_in[h, q], u * (16 * SLOTS))
                            v.tensor_copy(want[h, q][:, :], row_i[:, bass.ds(n * QUAD + q, 1), :].rearrange("p o s -> p (o s)")).then_inc(want_ready, 1)

                    def body(n, h, u):
                        if not (isinstance(u, int) and u == QUADS // 2 - 1 and h == 1):
                            name_rows(n + 1, 1 - h, u + h)
                        steps = Steps(dve, step_done, STEPS, n)
                        for j in range(SLOTS):
                            for q in range(QUAD):
                                if j == 0:
                                    dve.wait_ge(rows_in[h, q], (u + 1) * (16 * SLOTS))
                                    dve.wait_ge(x2r_in[h, q], (u + 1) * 16)
                                    wait(dve, o_ready, (n - 1) * QUAD + (q + 1))
                                else:
                                    steps.need((j - 1) * QUAD + q + 1)
                                w = weight[:, bass.ds(n * QUAD + q, 1), j:j + 1].rearrange("p o s -> p (o s)")
                                last = v.scalar_tensor_tensor(acc[q][:, :], rows4[h, q][:, j, :], w, (acc[q] if j else x2r[h, q])[:, :],
                                                              ALU.mult, ALU.add)
                                if j == SLOTS - 1:
                                    last.then_inc(rows_used, 1)
                                else:
                                    steps.done(last)
                        for q in range(QUAD):
                            dve.wait_ge(rows_used, n * QUAD + (q + 1))
                            steps.done(v.bn_stats(st4[:, q, :], acc[q][:, :]))
                        for q in range(QUAD):
                            steps.need((SLOTS - 1) * QUAD + q + 1)
                            settle(dve, settled)
                            steps.done(v.bn_aggr(mv4[:, q, :], st4[:, q, :]))
                        steps.need()
                        chain = (mv4[:, :, 1], ve[:, :], bits[:, :], rstd[:, :], ya[:, :], yb[:, :])
                        rsqrt_begin(steps, chain)
                        rsqrt_end(steps, chain)
                        steps.need()
                        for q in range(QUAD):
                            wait(dve, out_done[h, q], u * 16)
                            v.tensor_scalar(o_s[h, q][:, :], acc[q][:, :], mv4[:, q, 0:1], rstd[:, q:q + 1], ALU.subtract, ALU.mult).then_inc(o_ready, 1)

                    STEPS = (SLOTS + 1) * QUAD + RSQRT_STEPS
                    name_rows(0, 0, 0)
                    quads(dve, body)


_INS = ["xT", "x", "cT", "mask", "wq", "wk", "wv", "wo", "xwq", "xbq", "xwk", "xbk", "xwv", "xbv", "xwo", "xbo",
        "r0", "g0", "u0", "d0", "r1", "g1", "u1", "d1"]


def kernel(x, ctx_1024, mask_BxSxS2_ik1, L0_attn_w_q, L0_attn_w_k, L0_attn_w_v, L0_attn_w_o, L0_xattn_Wq, L0_xattn_bq,
           L0_xattn_Wk, L0_xattn_bk, L0_xattn_Wv, L0_xattn_bv, L0_xattn_Wo, L0_xattn_bo, L0_ffn_router_w0, L0_ffn_wg0,
           L0_ffn_wu0, L0_ffn_wd0, L0_ffn_router_w1, L0_ffn_wg1, L0_ffn_wu1, L0_ffn_wd1):
    import numpy as np
    import concourse.bacc as bacc
    from concourse.bass_utils import run_bass_kernel_spmd

    def by_partition(w):
        w = np.asarray(w)
        return np.ascontiguousarray(w.reshape(-1, P, w.shape[1]).transpose(1, 0, 2).reshape(P, -1))

    def tokens_last(a):
        a = np.asarray(a)
        return np.ascontiguousarray(a.reshape(a.shape[0], P, KC, P).transpose(0, 3, 2, 1).reshape(a.shape[0], P, KC * P))

    def flat_t(w):
        return np.asarray(w).reshape(HD, D).T

    def column(b):
        return np.ascontiguousarray(np.asarray(b).reshape(KC, P).T)

    def one_row(b):
        return np.asarray(b).reshape(1, D)

    arrays = dict(
        xT=tokens_last(x), x=np.asarray(x), cT=tokens_last(ctx_1024), mask=np.asarray(mask_BxSxS2_ik1),
        wq=by_partition(flat_t(L0_attn_w_q)), wk=by_partition(flat_t(L0_attn_w_k)), wv=by_partition(flat_t(L0_attn_w_v)),
        wo=by_partition(L0_attn_w_o),
        xwq=by_partition(np.asarray(L0_xattn_Wq).T), xbq=column(L0_xattn_bq), xwk=by_partition(np.asarray(L0_xattn_Wk).T),
        xbk=column(L0_xattn_bk), xwv=by_partition(np.asarray(L0_xattn_Wv).T), xbv=one_row(L0_xattn_bv),
        xwo=by_partition(np.asarray(L0_xattn_Wo).T), xbo=one_row(L0_xattn_bo),
        r0=np.asarray(L0_ffn_router_w0), g0=np.asarray(L0_ffn_wg0), u0=np.asarray(L0_ffn_wu0), d0=np.asarray(L0_ffn_wd0),
        r1=np.asarray(L0_ffn_router_w1), g1=np.asarray(L0_ffn_wg1), u1=np.asarray(L0_ffn_wu1), d1=np.asarray(L0_ffn_wd1))
    nc = bacc.Bacc("TRN2", target_bir_lowering=False, num_devices=1)
    aps = [nc.dram_tensor(n, arrays[n].shape, mybir.dt.from_np(arrays[n].dtype), kind="ExternalInput").ap() for n in _INS]
    out = nc.dram_tensor("out", tuple(x.shape), F32, kind="ExternalOutput").ap()
    decoder_layer(nc, *aps, out)
    result = run_bass_kernel_spmd(nc, [arrays], core_ids=[0])
    return result.results[0]["out"]
```

```python
from contextlib import ExitStack

import concourse.bass as bass
from concourse import mybir

F32 = mybir.dt.float32
BF16 = mybir.dt.bfloat16
I32 = mybir.dt.int32
U32 = mybir.dt.uint32
ALU = mybir.AluOpType
ACT = mybir.ActivationFunctionType
AX = mybir.AxisListType

P = 128
D = 256
KC = D // P
H, DH = 16, 64
HD = H * DH
PAIRS = H // 2
XH = 16
XD = D // XH
XPC = P // XD
QUARTERS = XPC // 2
GH = 4
NG = H // GH
E, TOPK, NGRP = 32, 2, 2
NE = E * NGRP
HID = 128
WCOL = KC * 2 * HID + D
HALF = E // 2
EPS = 1e-5
BIG = float(2.0 ** 100)
RSQRT_SEED = float(0x5F3759DF)
SLOTS = NGRP * TOPK


class When:

    def __init__(self, u, p, n, first, last, base=0):
        self.u, self.p, self.n, self.first, self.last, self.base = u, p, n, first, last, base
        assert base % n == 0

    def live(self, lag):
        return not isinstance(self.u, int) or self.first <= self.item(lag) < self.last

    def item(self, lag):
        return self.u * self.n + (self.p - lag - self.base)

    def slot(self, lag):
        return (self.p - lag) % self.n

    def turn(self, lag):
        return self.u + (self.p - lag - self.base) // self.n


def at(number, n, first, last):
    return When(number // n, number % n, n, first, last)


def wait(eng, sem, value):
    if isinstance(value, int) and value <= 0:
        return
    eng.wait_ge(sem, value)


def settle(eng, settled):
    eng.sem_inc(settled, 1)


class Steps:

    def __init__(self, eng, sem, size, item):
        self.eng, self.sem, self.base, self.size, self.n = eng, sem, item * size, size, 0

    def done(self, instruction):
        self.n += 1
        assert self.n <= self.size
        instruction.then_inc(self.sem, 1)

    def need(self, n=None):
        self.eng.wait_ge(self.sem, self.base + (self.n if n is None else n))


def spread(ap, axis, n):
    a = ap.unsqueeze(axis)
    shape = list(a.shape)
    shape[axis] = n
    return a.broadcast_to(shape)


JOBS = [
    (0, "q0", -1, 0), (0, "q1", -1, 0), (0, "xk", 1, 0),
    (1, "o2", 3, 0), (1, "rank", 4, D), (1, "o1", 1, 0),
    (2, "k0", -1, 0), (2, "k1", -1, 0), (2, "x1t", 1, 0), (2, "x2t", 3, D),
    (3, "v0", -1, 0), (3, "xq", 1, 0), (3, "route", 3, D), (3, "v1", -1, 0), (3, "xv", 1, 0),
]
JBANKS = 3
USE = [sum(1 for _, _, _, c in JOBS[:n + 1] if c == 0) - 1 for n in range(len(JOBS))]
USES = USE[-1] + 1
BANK = {job[1]: USE[n] % JBANKS for n, job in enumerate(JOBS)}
MOVES = {"k0": 2, "k1": 2}
assert USES % JBANKS == 0


def bank_before(t, n):
    for use in range(USE[n] - JBANKS, USE[n] - 4 * USES, -JBANKS):
        back = -(use // USES)
        found = [(name, t.item(lag + back) + 1) for m, (_, name, lag, _) in enumerate(JOBS)
                 if USE[m] == use % USES and t.live(lag + back)]
        if found:
            return found
    return []


def decoder_layer(nc, xT, x, cT, mask, wq, wk, wv, wo, xwq, xbq, xwk, xbk, xwv, xbv, xwo, xbo,
                  r0, g0, u0, d0, r1, g1, u1, d1, out):
    NB = x.shape[0]
    N = NB * P
    TILES = NB * TOPK + E
    NT = NGRP * TILES
    PACK = 4
    TA = -(-NT // (P * PACK)) * PACK
    x2_d = nc.dram_tensor("x2_d", (N, D), F32).ap()
    list_d = nc.dram_tensor("list_d", (NE * N, 1), I32).ap()
    y_d = [nc.dram_tensor(f"y{g}_d", (TILES * P, D), F32).ap() for g in range(NGRP)]
    acc_d = nc.dram_tensor("acc_d", (N, D), F32).ap()
    tab_d = nc.dram_tensor("tab_d", (P * TA // PACK,), I32).ap()

    keep = ExitStack()
    with keep:
        def tile(stack, name, shape, dt=F32):
            return stack.enter_context(nc.sbuf_tensor(name, shape, dt))

        def sem(name):
            return keep.enter_context(nc.semaphore(name))

        banks = [keep.enter_context(nc.psum_tensor(f"bank{i}", [P, 512], F32)) for i in range(8)]

        ident = tile(keep, "ident", [P, P])
        ones_b = tile(keep, "ones_b", [P, P], BF16)
        picked = tile(keep, "picked", [P, NE], BF16)
        expert = tile(keep, "expert", [P, NB, SLOTS])
        rank = tile(keep, "rank", [P, NB, SLOTS])
        weight = tile(keep, "weight", [P, NB, SLOTS])
        row_i = tile(keep, "row_i", [P, NB, SLOTS], I32)

        settled = sem("settled")

        def load_experts(eng, dst, first, gate, up, down, done):
            for k in range(KC):
                for j, w in enumerate((gate, up)):
                    eng.dma_start(dst[:, :, (2 * k + j) * HID:(2 * k + j + 1) * HID],
                                  w[first:first + HALF, k * P:(k + 1) * P, :].rearrange("e p h -> p e h")).then_inc(done, 16)
            eng.dma_start(dst[:, :, KC * 2 * HID:WCOL],
                          down[first:first + HALF, :, :].rearrange("e p d -> p e d")).then_inc(done, 16)

        MOE_LOAD = 16 * (2 * KC + 1)
        RSQRT_STEPS = 12

        def newton(steps, tiles, turns):
            var, ve, bits, y, a, b = tiles
            v = nc.vector
            for _ in range(turns):
                steps.need()
                steps.done(v.tensor_tensor(a, y, y, ALU.mult))
                steps.need()
                steps.done(v.scalar_tensor_tensor(b, a, -0.5, ve, ALU.mult, ALU.mult))
                steps.need()
                steps.done(v.scalar_tensor_tensor(y, b, 1.5, y, ALU.add, ALU.mult))

        def rsqrt_begin(steps, tiles):
            var, ve, bits, y, a, b = tiles
            v = nc.vector
            steps.done(v.tensor_scalar(ve, var, EPS, None, ALU.add))
            steps.need()
            steps.done(v.tensor_single_scalar(bits.bitcast(I32), ve.bitcast(I32), 1, op=ALU.arith_shift_right))
            steps.need()
            steps.done(v.tensor_scalar(y.bitcast(I32), bits.bitcast(I32), -1.0, RSQRT_SEED, ALU.mult, ALU.add))
            newton(steps, tiles, 1)

        def rsqrt_end(steps, tiles):
            newton(steps, tiles, 2)

        with ExitStack() as one:
            def sb(name, shape, dt=F32):
                return tile(one, name, shape, dt)

            wq_s, wk_s, wv_s = (sb(n, [P, KC, HD]) for n in ("wq_s", "wk_s", "wv_s"))
            wo_s = sb("wo_s", [P, PAIRS, D])
            xwq_s, xwk_s, xwv_s, xwo_s = (sb(n, [P, KC, D]) for n in ("xwq_s", "xwk_s", "xwv_s", "xwo_s"))
            xbq_s, xbk_s = sb("xbq_s", [P, KC]), sb("xbk_s", [P, KC])
            bias_row = sb("bias_row", [1, 2, D])
            xbv_s, xbo_s = sb("xbv_s", [P, D]), sb("xbo_s", [P, D])
            router_s = sb("router_s", [P, KC, NE])
            causal = sb("causal", [P, P])
            before_b = sb("before_b", [P, P], BF16)
            own_head = sb("own_head", [P, XPC])
            iota_e = sb("iota_e", [P, E])
            group_first = sb("group_first", [P, SLOTS])
            token_no = sb("token_no", [P, NB], I32)
            zeros = sb("zeros", [P, 512], I32)

            xT_s = [sb(f"xT{p}", [P, KC, P]) for p in (0, 1)]
            x_s = [sb(f"x{p}", [P, D]) for p in (0, 1)]
            cT_s = [sb(f"cT{p}", [P, KC, P]) for p in (0, 1)]
            mask_s = [sb(f"mask{p}", [P, P], I32) for p in (0, 1)]
            xmask = [sb(f"xmask{p}", [P, P]) for p in (0, 1)]
            qT = [sb(f"qT{p}", [P, PAIRS, P]) for p in (0, 1)]
            kD = [sb(f"kD{p}", [P, PAIRS, 2 * P]) for p in (0, 1)]
            v_s = [sb(f"v{p}", [P, HD]) for p in (0, 1)]
            xqT = [sb(f"xqT{p}", [P, KC, P]) for p in (0, 1)]
            xkD = [sb(f"xkD{p}", [P, KC, XPC, P]) for p in (0, 1)]
            xvD = [sb(f"xvD{p}", [P, KC, QUARTERS, 2, 2 * XD]) for p in (0, 1)]
            prob = [sb(f"prob{p}", [P, GH, P]) for p in (0, 1)]
            xprob = [sb(f"xprob{p}", [P, GH, P]) for p in (0, 1)]
            probT, xprobT = sb("probT", [P, GH, P]), sb("xprobT", [P, GH, P])
            negmax = [sb(f"negmax{p}", [P, GH]) for p in (0, 1)]
            xnegmax = [sb(f"xnegmax{p}", [P, GH]) for p in (0, 1)]
            total = [sb(f"total{p}", [P, GH]) for p in (0, 1)]
            xtotal = [sb(f"xtotal{p}", [P, GH]) for p in (0, 1)]
            inv, xinv = sb("inv", [P, GH]), sb("xinv", [P, GH])
            yT, xyT = sb("yT", [P, PAIRS, P]), sb("xyT", [P, KC, P])
            sum1, sum2 = sb("sum1", [P, D]), sb("sum2", [P, D])
            stats, mv = sb("stats", [P, 2, 6]), sb("mv", [P, 2, 2])
            rs = sb("rs", [P, 2, 5])
            x1 = [sb(f"x1_{p}", [P, D]) for p in (0, 1)]
            x1b = [sb(f"x1b_{p}", [P, D]) for p in (0, 1)]
            x2 = [sb(f"x2_{p}", [P, D]) for p in (0, 1)]
            x1T, x2T = sb("x1T", [P, KC, P]), sb("x2T", [P, KC, P])
            top8, top8i = sb("top8", [P, NGRP, 8]), sb("top8i", [P, NGRP, 8], U32)
            below = sb("below", [P, NE + NGRP])
            soft = sb("soft", [P, NE + NGRP])
            soft_sum, soft_inv = sb("soft_sum", [P, NGRP]), sb("soft_inv", [P, NGRP])
            choice = sb("choice", [P, NGRP, TOPK])
            hot = sb("hot", [P, NGRP, TOPK, E])
            hot_b = sb("hot_b", [P, NGRP, E], BF16)
            hot_rank = sb("hot_rank", [P, NGRP, TOPK, E])
            list_row = sb("list_row", [P, SLOTS])
            place = [sb(f"place{p}", [P, SLOTS], I32) for p in (0, 1)]
            token = [sb(f"token{p}", [P, 1], I32) for p in (0, 1)]

            S, XS, T, XT, PV, JB = banks[0], banks[1], banks[2], banks[3], banks[4], banks[5:8]
            SELF, CROSS = slice(0, 2 * P), slice(2 * P, 3 * P)

            weights_in = sem("weights_in")
            consts = sem("consts")
            zeroed = sem("zeroed")
            list_clear = sem("list_clear")
            xT_in, x_in, cT_in, mask_in = ([sem(f"{n}_in{p}") for p in (0, 1)] for n in ("xT", "x", "cT", "mask"))
            x2_out = [sem(f"x2_out{p}") for p in (0, 1)]
            placed = [sem(f"placed{p}") for p in (0, 1)]
            scores, xscores = sem("scores"), sem("xscores")
            maxed, xmaxed = sem("maxed"), sem("xmaxed")
            exped, xexped = sem("exped"), sem("xexped")
            normed, xnormed = sem("normed"), sem("xnormed")
            turned, xturned = sem("turned"), sem("xturned")
            probT_in, xprobT_in = sem("probT_in"), sem("xprobT_in")
            mixed, xmixed = sem("mixed"), sem("xmixed")
            yT_in, xyT_in = sem("yT_in"), sem("xyT_in")
            made = {n: sem(f"made_{n}") for _, n, _, _ in JOBS}
            moved = {n: sem(f"moved_{n}") for _, n, _, _ in JOBS}
            x1_ready, x1b_ready, x2_ready = sem("x1_ready"), sem("x1b_ready"), sem("x2_ready")
            xmask_ready = sem("xmask_ready")
            soft_ready = sem("soft_ready")
            hot_ready, picked_ready = sem("hot_ready"), sem("picked_ready")
            place_ready, list_row_ready = sem("place_ready"), sem("list_row_ready")
            inv_ready, xinv_ready = sem("inv_ready"), sem("xinv_ready")
            place_step, norm1_step, norm2_step, rsqrt_step, route_step, weigh_step = (
                sem(n) for n in ("place_step", "norm1_step", "norm2_step", "rsqrt_step", "route_step", "weigh_step"))

            W_IN = 16 * 16

            def pipeline(eng, iteration):
                for i in range(-1, 6):
                    iteration(at(i, 2, 0, NB))
                with eng.Fori(3, NB // 2 - 1) as u:
                    for p in (0, 1):
                        iteration(When(u, p, 2, 0, NB))
                for i in range(NB - 2, NB + 4):
                    iteration(at(i, 2, 0, NB))

            def behind(s, lag):
                return (lag, s - 1) if s else (lag + 1, NG - 1)

            with nc.Block() as block:
                @block.sync
                def _(sp):
                    sp.dma_start(xT_s[0][:, :, :].rearrange("p k t -> p (k t)"), xT[0, :, :]).then_inc(xT_in[0], 16)
                    for dst, src in ((wq_s, wq), (wk_s, wk), (wv_s, wv), (wo_s, wo), (xwq_s, xwq), (xwk_s, xwk),
                                     (xwv_s, xwv), (xwo_s, xwo)):
                        sp.dma_start(dst[:, :, :].rearrange("p k n -> p (k n)"), src).then_inc(weights_in, 16)
                    for dst, src in ((xbq_s[:, :], xbq), (xbk_s[:, :], xbk)):
                        sp.dma_start(dst, src).then_inc(weights_in, 16)
                    sp.dma_start(bias_row[0:1, 0, :], xbv).then_inc(weights_in, 16)
                    sp.dma_start(bias_row[0:1, 1, :], xbo).then_inc(weights_in, 16)
                    for k in range(KC):
                        for g, r in enumerate((r0, r1)):
                            sp.dma_start(router_s[:, k, g * E:(g + 1) * E], r[k * P:(k + 1) * P, :]).then_inc(weights_in, 16)
                    sp.wait_ge(zeroed, 1)
                    clear = list_d.rearrange("(c p n) o -> c p (n o)", p=P, n=min(512, NE * N // P))
                    for c in range(clear.shape[0]):
                        sp.dma_start(clear[c, :, :], zeros[:, 0:clear.shape[2]]).then_inc(list_clear, 16)

                    def iteration(t):
                        if t.live(-2):
                            wait(sp, made["v1"], t.item(0) + 1)
                            sp.dma_start(xT_s[t.slot(-2)][:, :, :].rearrange("p k t -> p (k t)"),
                                         xT[bass.ds(t.item(-2), 1), :, :].rearrange("o p n -> (o p) n")).then_inc(xT_in[t.slot(-2)], 16)
                        if t.live(0):
                            wait(sp, made["xv"], t.item(2) + 1)
                            sp.dma_start(cT_s[t.slot(0)][:, :, :].rearrange("p k t -> p (k t)"),
                                         cT[bass.ds(t.item(0), 1), :, :].rearrange("o p n -> (o p) n")).then_inc(cT_in[t.slot(0)], 16)
                            wait(sp, xmask_ready, t.item(2) + 1)
                            sp.dma_start(mask_s[t.slot(0)][:, :],
                                         mask[bass.ds(t.item(0), 1), :, :].rearrange("o p n -> (o p) n")).then_inc(mask_in[t.slot(0)], 16)
                        if t.live(-1):
                            wait(sp, x1_ready, t.item(1) + 1)
                            sp.dma_start(x_s[t.slot(-1)][:, :],
                                         x[bass.ds(t.item(-1), 1), :, :].rearrange("o p n -> (o p) n")).then_inc(x_in[t.slot(-1)], 16)
                        if t.live(3):
                            sp.wait_ge(x2_ready, t.item(3) + 1)
                            sp.dma_start(x2_d[bass.ds(t.item(3) * P, P), :], x2[t.slot(3)][:, :]).then_inc(x2_out[t.slot(3)], 16)

                    pipeline(sp, iteration)
                    for p in (0, 1):
                        sp.wait_ge(x2_out[p], 16 * (NB // 2))

                @block.gpsimd
                def _(pool):
                    nc.gpsimd.memset(zeros[:, :], 0).then_inc(zeroed, 1)
                    nc.gpsimd.memset(ident[:, :], 0.0).then_inc(consts, 1)
                    nc.gpsimd.memset(ones_b[:, :], 1.0).then_inc(consts, 1)
                    nc.gpsimd.memset(causal[:, :], 0.0).then_inc(consts, 1)
                    nc.gpsimd.memset(before_b[:, :], 1.0).then_inc(consts, 1)
                    nc.gpsimd.memset(own_head[:, :], 1.0).then_inc(consts, 1)
                    nc.gpsimd.iota(token_no[:, :], pattern=[[P, NB]], base=0, channel_multiplier=1).then_inc(consts, 1)
                    nc.gpsimd.iota(iota_e[:, :], pattern=[[1, E]], base=0, channel_multiplier=0,
                                   allow_small_or_imprecise_dtypes=True).then_inc(consts, 1)
                    nc.gpsimd.iota(group_first[:, :], pattern=[[E, NGRP], [0, TOPK]], base=0, channel_multiplier=0,
                                   allow_small_or_imprecise_dtypes=True).then_inc(consts, 1)
                    for p in (0, 1):
                        nc.gpsimd.memset(kD[p][:, :, :], 0.0).then_inc(consts, 1)
                        nc.gpsimd.memset(xvD[p][:, :, :, :, :], 0.0).then_inc(consts, 1)
                    nc.gpsimd.memset(picked[:, :], 0.0).then_inc(consts, 1)
                    nc.gpsimd.memset(mv[:, :, :], 1.0).then_inc(consts, 1)
                    pool.wait_ge(consts, 14)
                    nc.gpsimd.affine_select(out=ident[:, :], in_=ident[:, :], compare_op=ALU.not_equal, fill=1.0,
                                            base=0, pattern=[[-1, P]], channel_multiplier=1).then_inc(consts, 1)
                    nc.gpsimd.affine_select(out=causal[:, :], in_=causal[:, :], compare_op=ALU.is_ge, fill=-BIG,
                                            base=0, pattern=[[-1, P]], channel_multiplier=1).then_inc(consts, 1)
                    nc.gpsimd.affine_select(out=before_b[:, :], in_=before_b[:, :], compare_op=ALU.is_gt, fill=0.0,
                                            base=0, pattern=[[1, P]], channel_multiplier=-1).then_inc(consts, 1)
                    nc.gpsimd.affine_select(out=own_head[:, :], in_=own_head[:, :], compare_op=ALU.is_ge, fill=0.0,
                                            base=0, pattern=[[-XD, XPC]], channel_multiplier=1).then_inc(consts, 1)
                    pool.wait_ge(consts, 18)
                    nc.gpsimd.affine_select(out=own_head[:, :], in_=own_head[:, :], compare_op=ALU.is_ge, fill=0.0,
                                            base=XD - 1, pattern=[[XD, XPC]], channel_multiplier=-1).then_inc(consts, 1)
                    pool.wait_ge(weights_in, W_IN)
                    nc.gpsimd.partition_broadcast(xbv_s[:, :], bias_row[0:1, 0, :]).then_inc(consts, 1)
                    nc.gpsimd.partition_broadcast(xbo_s[:, :], bias_row[0:1, 1, :]).then_inc(consts, 1)
                    pool.wait_ge(consts, 21)
                    pool.wait_ge(list_clear, 16 * (NE * N // P // min(512, NE * N // P)))

                    def iteration(t):
                        if t.live(4):
                            pool.wait_ge(place_ready, t.item(4) + 1)
                            settle(pool, settled)
                            p = t.slot(4)
                            for j in range(SLOTS):
                                nc.gpsimd.indirect_dma_start(
                                    list_d[:, :], bass.IndirectOffsetOnAxis(ap=place[p][:, j:j + 1].bitcast(U32), axis=0),
                                    token[p][:, :], None).then_inc(placed[p], 16)
                        if t.live(1):
                            pool.wait_ge(x1_ready, t.item(1) + 1)
                            nc.gpsimd.tensor_tensor(x1b[t.slot(1)][:, :], x1[t.slot(1)][:, :], xbo_s[:, :], ALU.add).then_inc(x1b_ready, 1)

                    pipeline(pool, iteration)
                    for p in (0, 1):
                        pool.wait_ge(placed[p], 16 * SLOTS * (NB // 2))

                @block.tensor
                def _(pe):
                    pe.wait_ge(weights_in, W_IN)
                    pe.wait_ge(consts, 21)

                    def chunks(out_ap, lhs, rhs, n=KC):
                        for k in range(n):
                            last = nc.tensor.matmul(out_ap, lhs(k), rhs(k), start=(k == 0), stop=(k == n - 1))
                        return last

                    def job(t, n):
                        step, name, lag, col = JOBS[n]
                        if not t.live(lag):
                            return
                        for prior, count in bank_before(t, n):
                            wait(pe, moved[prior], count * MOVES.get(prior, 1))
                        o, p = JB[BANK[name]][:, col:], t.slot(lag)
                        if name in ("q0", "q1", "k0", "k1"):
                            w = wq_s if name[0] == "q" else wk_s
                            pe.wait_ge(xT_in[p], (t.turn(lag) + 1) * 16)
                            for c in range(4):
                                f = (4 * int(name[1]) + c) * P
                                last = chunks(o[:, c * P:(c + 1) * P], lambda k: w[:, k, f:f + P], lambda k: xT_s[p][:, k, :])
                        elif name in ("v0", "v1"):
                            f = 512 * int(name[1])
                            last = chunks(o[:, :], lambda k: xT_s[p][:, k, :], lambda k: wv_s[:, k, f:f + 512])
                        elif name == "o1":
                            pe.wait_ge(yT_in, (t.item(lag) + 1) * NG)
                            last = chunks(o[:, 0:D], lambda c: yT[:, c, :], lambda c: wo_s[:, c, :], PAIRS)
                        elif name == "o2":
                            pe.wait_ge(xyT_in, (t.item(lag) + 1) * NG)
                            last = chunks(o[:, 0:D], lambda c: xyT[:, c, :], lambda c: xwo_s[:, c, :])
                        elif name in ("x1t", "x2t"):
                            src, ready = (x1, x1_ready) if name == "x1t" else (x2, x2_ready)
                            pe.wait_ge(ready, t.item(lag) + 1)
                            for k in range(KC):
                                last = nc.tensor.transpose(o[:, k * P:(k + 1) * P], src[p][:, k * P:(k + 1) * P], ident[:, :])
                        elif name in ("xq", "xk"):
                            if name == "xq":
                                pe.wait_ge(moved["x1t"], t.item(lag) + 1)
                                w, r = xwq_s, x1T
                            else:
                                pe.wait_ge(cT_in[p], (t.turn(lag) + 1) * 16)
                                w, r = xwk_s, cT_s[p]
                            for m in range(KC):
                                last = chunks(o[:, m * P:(m + 1) * P], lambda k: w[:, k, m * P:(m + 1) * P], lambda k: r[:, k, :])
                        elif name == "route":
                            pe.wait_ge(moved["x2t"], t.item(lag) + 1)
                            last = chunks(o[:, 0:NE], lambda k: x2T[:, k, :], lambda k: router_s[:, k, :])
                        elif name == "rank":
                            pe.wait_ge(hot_ready, t.item(lag) + 1)
                            wait(pe, picked_ready, t.item(lag))
                            nc.tensor.matmul(o[:, 0:NE], before_b[:, :], hot_b[:, :, :].rearrange("p g e -> p (g e)"), start=True, stop=False)
                            last = nc.tensor.matmul(o[:, 0:NE], ones_b[:, :], picked[:, :], start=False, stop=True)
                        else:
                            last = chunks(o[:, 0:D], lambda k: cT_s[p][:, k, :], lambda k: xwv_s[:, k, :])
                        last.then_inc(made[name], 1)

                    def iteration(t):
                        for s in range(NG):
                            if t.live(0):
                                p = t.slot(0)
                                if s == 0:
                                    for n in ("q0", "q1", "k0", "k1"):
                                        pe.wait_ge(moved[n], (t.item(0) + 1) * MOVES.get(n, 1))
                                wait(pe, maxed, t.item(0) * NG + s)
                                for j in range(GH // 2):
                                    c = s * GH // 2 + j
                                    last = nc.tensor.matmul(S[:, j * 2 * P:(j + 1) * 2 * P], qT[p][:, c, :], kD[p][:, c, :],
                                                            start=True, stop=True)
                                last.then_inc(scores, 1)
                            if t.live(2):
                                p = t.slot(2)
                                if s == 0:
                                    pe.wait_ge(moved["xq"], t.item(2) + 1)
                                    pe.wait_ge(moved["xk"], t.item(2) + 1)
                                wait(pe, xmaxed, t.item(2) * NG + s)
                                c, j = divmod(s * GH, XPC)
                                nc.tensor.matmul(XS[:, :], xqT[p][:, c, :], xkD[p][:, c, j:j + GH, :].rearrange("p h k -> p (h k)"),
                                                 start=True, stop=True).then_inc(xscores, 1)
                            lag, g = behind(s, 0)
                            xlag, xg = behind(s, 2)
                            if t.live(lag):
                                pe.wait_ge(normed, t.item(lag) * NG + (g + 1))
                                wait(pe, probT_in, t.item(lag) * NG + g)
                                for h in range(GH):
                                    last = nc.tensor.transpose(T[:, h * P:(h + 1) * P], prob[g % 2][:, h, :], ident[:, :])
                                last.then_inc(turned, 1)
                            if t.live(xlag):
                                pe.wait_ge(xnormed, t.item(xlag) * NG + (xg + 1))
                                wait(pe, xprobT_in, t.item(xlag) * NG + xg)
                                for h in range(GH):
                                    last = nc.tensor.transpose(XT[:, h * P:(h + 1) * P], xprob[xg % 2][:, h, :], ident[:, :])
                                last.then_inc(xturned, 1)
                            for n, (step, *_) in enumerate(JOBS):
                                if step == s:
                                    job(t, n)
                            if t.live(lag):
                                pe.wait_ge(probT_in, t.item(lag) * NG + (g + 1))
                                wait(pe, yT_in, t.item(lag) * NG + g)
                            if t.live(xlag):
                                pe.wait_ge(xprobT_in, t.item(xlag) * NG + (xg + 1))
                                wait(pe, xyT_in, t.item(xlag) * NG + xg)
                            if t.live(lag):
                                if g == 0:
                                    pe.wait_ge(moved["v0"], t.item(lag) + 1)
                                    pe.wait_ge(moved["v1"], t.item(lag) + 1)
                                v = v_s[t.slot(lag)]
                                for h in range(GH):
                                    f = (g * GH + h) * DH
                                    r = DH * (h % 2)
                                    last = nc.tensor.matmul(PV[r:r + DH, (h // 2) * P:(h // 2 + 1) * P], v[:, f:f + DH], probT[:, h, :],
                                                            start=True, stop=True)
                                last.then_inc(mixed, 1)
                            if t.live(xlag):
                                if xg == 0:
                                    pe.wait_ge(moved["xv"], t.item(xlag) + 1)
                                for j in (0, 1):
                                    for quarter in range(GH // 2):
                                        c, n = divmod(xg * GH // 2 + quarter, QUARTERS)
                                        r = 2 * XD * n
                                        last = nc.tensor.matmul(PV[r:r + 2 * XD, CROSS], xvD[t.slot(xlag)][:, c, n, j, :], xprobT[:, 2 * quarter + j, :],
                                                                start=(j == 0), stop=(j == 1))
                                last.then_inc(xmixed, 1)

                    pipeline(pe, iteration)

                @block.scalar
                def _(act):
                    act.wait_ge(consts, 21)

                    def exponentials(dst, src_bias, acc):
                        for h in range(GH):
                            last = nc.scalar.activation(dst[:, h, :], dst[:, h, :], ACT.Exp, bias=src_bias[:, h:h + 1], scale=-1.0,
                                                        accum_out=acc[:, h:h + 1])
                        return last

                    def iteration(t):
                        for s in range(NG):
                            lag, g = behind(s, 0)
                            xlag, xg = behind(s, 2)
                            if t.live(0):
                                act.wait_ge(maxed, t.item(0) * NG + (s + 1))
                                exponentials(prob[s % 2], negmax[s % 2], total[s % 2]).then_inc(exped, 1)
                            if t.live(lag):
                                act.wait_ge(turned, t.item(lag) * NG + (g + 1))
                                nc.scalar.copy(probT[:, :, :].rearrange("p h q -> p (h q)"), T[:, :]).then_inc(probT_in, 1)
                            if t.live(xlag):
                                act.wait_ge(xturned, t.item(xlag) * NG + (xg + 1))
                                nc.scalar.copy(xprobT[:, :, :].rearrange("p h q -> p (h q)"), XT[:, :]).then_inc(xprobT_in, 1)
                            if s == 2 and t.live(-1):
                                for n in (0, 1):
                                    act.wait_ge(made[f"k{n}"], t.item(-1) + 1)
                                    nc.scalar.copy(kD[t.slot(-1)][0:DH, 4 * n:4 * n + 4, 0:P],
                                                   JB[BANK[f"k{n}"]][0:DH, :].rearrange("p (c k) -> p c k", c=4)).then_inc(moved[f"k{n}"], 1)
                            if t.live(2):
                                act.wait_ge(xmaxed, t.item(2) * NG + (s + 1))
                                exponentials(xprob[s % 2], xnegmax[s % 2], xtotal[s % 2]).then_inc(xexped, 1)
                            if s == 2:
                                joined = [(n, lg) for n, lg in (("x1t", 1), ("x2t", 3)) if t.live(lg)]
                                for n, lg in joined:
                                    act.wait_ge(made[n], t.item(lg) + 1)
                                for n, lg in joined:
                                    dst, c = (x1T, 0) if n == "x1t" else (x2T, D)
                                    nc.scalar.copy(dst[:, :, :].rearrange("p k t -> p (k t)"), JB[BANK[n]][:, c:c + D]).then_inc(moved[n], 1)
                            if s == 3:
                                if t.live(-1):
                                    act.wait_ge(made["v0"], t.item(-1) + 1)
                                    nc.scalar.copy(v_s[t.slot(-1)][:, 0:512], JB[BANK["v0"]][:, :]).then_inc(moved["v0"], 1)
                                if t.live(3):
                                    act.wait_ge(moved["route"], t.item(3) + 1)
                                    nc.scalar.activation(soft[:, :], below[:, :], ACT.Exp).then_inc(soft_ready, 1)
                                if t.live(-1):
                                    act.wait_ge(made["v1"], t.item(-1) + 1)
                                    nc.scalar.copy(v_s[t.slot(-1)][:, 512:1024], JB[BANK["v1"]][:, :]).then_inc(moved["v1"], 1)
                            if t.live(lag):
                                act.wait_ge(mixed, t.item(lag) * NG + (g + 1))
                            if t.live(xlag):
                                act.wait_ge(xmixed, t.item(xlag) * NG + (xg + 1))
                            if t.live(lag):
                                nc.scalar.copy(yT[:, 2 * g:2 * g + 2, :].rearrange("p c q -> p (c q)"), PV[:, SELF]).then_inc(yT_in, 1)
                            if t.live(xlag):
                                half = slice(xg % 2 * P // 2, (xg % 2 + 1) * P // 2)
                                nc.scalar.copy(xyT[half, xg // 2, :], PV[half, CROSS]).then_inc(xyT_in, 1)

                    pipeline(act, iteration)

                @block.vector
                def _(dve):
                    dve.wait_ge(consts, 21)

                    def masked(dst, bank, bias, least):
                        for h in range(GH):
                            last = nc.vector.tensor_tensor_reduce(dst[:, h, :], bank[:, h * P:(h + 1) * P], bias[:, :], -1.0, float("inf"),
                                                                  ALU.add, ALU.min, least[:, h:h + 1])
                        return last

                    def normalise(t, s, between=None):
                        if t.live(0):
                            dve.wait_ge(exped, t.item(0) * NG + (s + 1))
                            nc.vector.reciprocal(inv[:, :], total[s % 2][:, :]).then_inc(inv_ready, 1)
                            dve.wait_ge(inv_ready, t.item(0) * NG + (s + 1))
                            nc.vector.tensor_tensor(prob[s % 2][:, :, :], prob[s % 2][:, :, :], spread(inv[:, :], 2, P), ALU.mult).then_inc(normed, 1)
                        if between:
                            between()
                        if t.live(2):
                            dve.wait_ge(xexped, t.item(2) * NG + (s + 1))
                            nc.vector.reciprocal(xinv[:, :], xtotal[s % 2][:, :]).then_inc(xinv_ready, 1)
                            dve.wait_ge(xinv_ready, t.item(2) * NG + (s + 1))
                            nc.vector.tensor_tensor(xprob[s % 2][:, :, :], xprob[s % 2][:, :, :], spread(xinv[:, :], 2, P), ALU.mult).then_inc(xnormed, 1)

                    def cross_keys(t, m):
                        if t.live(1):
                            dve.wait_ge(made["xk"], t.item(1) + 1)
                            last = nc.vector.scalar_tensor_tensor(
                                xkD[t.slot(1)][:, m, :, :], spread(JB[BANK["xk"]][:, m * P:(m + 1) * P], 1, XPC), xbk_s[:, m:m + 1],
                                spread(own_head[:, :], 2, P), ALU.add, ALU.mult)
                            if m == KC - 1:
                                last.then_inc(moved["xk"], 1)

                    def norms_begin(t):
                        two_, one_, four = t.live(3), t.live(1), t.live(4)
                        if two_:
                            dve.wait_ge(made["o2"], t.item(3) + 1)
                        if four:
                            dve.wait_ge(made["rank"], t.item(4) + 1)
                        if two_:
                            steps2 = Steps(dve, norm2_step, 2, t.item(3))
                            dve.wait_ge(x1b_ready, t.item(3) + 1)
                            nc.vector.tensor_tensor(sum2[:, :], JB[BANK["o2"]][:, 0:D], x1b[t.slot(3)][:, :], ALU.add).then_inc(moved["o2"], 1)
                        if four:
                            nc.vector.tensor_tensor(hot_rank[:, :, :, :], hot[:, :, :, :],
                                                    spread(JB[BANK["rank"]][:, D:D + NE].rearrange("p (g e) -> p g e", g=NGRP), 2, TOPK),
                                                    ALU.mult).then_inc(moved["rank"], 1)
                        if two_:
                            dve.wait_ge(moved["o2"], t.item(3) + 1)
                            steps2.done(nc.vector.bn_stats(stats[:, 1, :], sum2[:, :]))
                        if one_:
                            steps1 = Steps(dve, norm1_step, 2, t.item(1))
                            dve.wait_ge(made["o1"], t.item(1) + 1)
                            dve.wait_ge(x_in[t.slot(1)], (t.turn(1) + 1) * 16)
                            nc.vector.tensor_tensor(sum1[:, :], JB[BANK["o1"]][:, 0:D], x_s[t.slot(1)][:, :], ALU.add).then_inc(moved["o1"], 1)
                        if two_:
                            steps2.need()
                            settle(dve, settled)
                            steps2.done(nc.vector.bn_aggr(mv[:, 1, :], stats[:, 1, :]))
                        if one_:
                            dve.wait_ge(moved["o1"], t.item(1) + 1)
                            steps1.done(nc.vector.bn_stats(stats[:, 0, :], sum1[:, :]))
                            steps1.need()
                            settle(dve, settled)
                            steps1.done(nc.vector.bn_aggr(mv[:, 0, :], stats[:, 0, :]))
                        if one_ or two_:
                            if two_:
                                steps2.need()
                            if one_:
                                steps1.need()
                            steps = Steps(dve, rsqrt_step, RSQRT_STEPS, t.item(1))
                            rsqrt_begin(steps, (mv[:, :, 1], *(rs[:, :, c] for c in range(5))))
                            return steps

                    def norms_end(t, steps):
                        two_, one_ = t.live(3), t.live(1)
                        if one_ or two_:
                            rsqrt_end(steps, (mv[:, :, 1], *(rs[:, :, c] for c in range(5))))
                            steps.need()
                        if two_:
                            wait(dve, x2_out[t.slot(3)], t.turn(3) * 16)
                            nc.vector.tensor_scalar(x2[t.slot(3)][:, :], sum2[:, :], mv[:, 1, 0:1], rs[:, 1, 2:3],
                                                    ALU.subtract, ALU.mult).then_inc(x2_ready, 1)
                        if one_:
                            nc.vector.tensor_scalar(x1[t.slot(1)][:, :], sum1[:, :], mv[:, 0, 0:1], rs[:, 0, 2:3],
                                                    ALU.subtract, ALU.mult).then_inc(x1_ready, 1)

                    def place_tokens(t):
                        if not t.live(4):
                            return
                        b, p = t.item(4), t.slot(4)
                        steps = Steps(dve, place_step, 1, b)
                        rank_b = rank[:, bass.ds(b, 1), :].rearrange("p o s -> p (o s)")
                        nc.vector.tensor_tensor(picked[:, :], picked[:, :], hot_b[:, :, :].rearrange("p g e -> p (g e)"), ALU.add).then_inc(picked_ready, 1)
                        dve.wait_ge(moved["rank"], b + 1)
                        steps.done(nc.vector.tensor_reduce(rank_b, hot_rank[:, :, :, :].rearrange("p g k e -> p (g k) e"), AX.X, ALU.add))
                        wait(dve, placed[p], t.turn(4) * 16 * SLOTS)
                        nc.vector.tensor_copy(token[p][:, :], token_no[:, bass.ds(b, 1)])
                        steps.need()
                        dve.wait_ge(list_row_ready, b + 1)
                        nc.vector.tensor_tensor(place[p][:, :], list_row[:, :], rank_b, ALU.add).then_inc(place_ready, 1)

                    def top_two(t):
                        if not t.live(3):
                            return
                        steps = Steps(dve, route_step, 6, t.item(3))
                        dve.wait_ge(made["route"], t.item(3) + 1)
                        settle(dve, settled)
                        lg = JB[BANK["route"]][:, D:D + NE].rearrange("p (g e) -> p g e", g=NGRP)
                        for g in range(NGRP):
                            steps.done(nc.vector.max(top8[:, g, :], lg[:, g, :]))
                        steps.need()
                        settle(dve, settled)
                        for g in range(NGRP):
                            steps.done(nc.vector.max_index(top8i[:, g, :], top8[:, g, :], lg[:, g, :]))
                        steps.done(nc.vector.tensor_tensor(below[:, NE:NE + NGRP], top8[:, :, 1], top8[:, :, 0], ALU.subtract))
                        nc.vector.tensor_tensor(below[:, 0:NE].rearrange("p (g e) -> p g e", g=NGRP), lg,
                                                top8[:, :, 0:1].broadcast_to([P, NGRP, E]), ALU.subtract).then_inc(moved["route"], 1)
                        steps.need(4)
                        steps.done(nc.vector.tensor_copy(choice[:, :, :], top8i[:, :, 0:TOPK]))

                    def weigh(t):
                        if not t.live(3):
                            return
                        b = t.item(3)
                        steps = Steps(dve, weigh_step, 4, b)
                        of_batch = expert[:, bass.ds(b, 1), :].rearrange("p o s -> p (o s)")
                        w_batch = weight[:, bass.ds(b, 1), :].rearrange("p o (g k) -> p (o g) k", g=NGRP)
                        dve.wait_ge(route_step, b * 6 + 6)
                        steps.done(nc.vector.tensor_tensor(hot[:, :, :, :].rearrange("p g k e -> p (g k) e"), spread(iota_e[:, :], 1, SLOTS),
                                                           spread(choice[:, :, :].rearrange("p g k -> p (g k)"), 2, E), ALU.is_equal))
                        dve.wait_ge(soft_ready, b + 1)
                        steps.done(nc.vector.tensor_reduce(soft_sum[:, :], soft[:, 0:NE].rearrange("p (g e) -> p g e", g=NGRP), AX.X, ALU.add))
                        steps.done(nc.vector.tensor_tensor(of_batch, choice[:, :, :].rearrange("p g k -> p (g k)"), group_first[:, :], ALU.add))
                        steps.need(1)
                        nc.vector.tensor_tensor(hot_b[:, :, :], hot[:, :, 0, :], hot[:, :, 1, :], ALU.add).then_inc(hot_ready, 1)
                        steps.need(2)
                        steps.done(nc.vector.reciprocal(soft_inv[:, :], soft_sum[:, :]))
                        steps.need(3)
                        nc.vector.tensor_scalar(list_row[:, :], of_batch, float(N), None, ALU.mult).then_inc(list_row_ready, 1)
                        steps.need(4)
                        nc.vector.tensor_scalar(w_batch[:, :, 0], soft_inv[:, :], 1.0 / NGRP, None, ALU.mult)
                        nc.vector.scalar_tensor_tensor(w_batch[:, :, 1], soft[:, NE:NE + NGRP], 1.0 / NGRP, soft_inv[:, :], ALU.mult, ALU.mult)

                    def iteration(t):
                        for s in range(NG):
                            if t.live(0):
                                dve.wait_ge(scores, t.item(0) * NG + (s + 1))
                                wait(dve, turned, t.item(0) * NG + (s - 1))
                                settle(dve, settled)
                                masked(prob[s % 2], S, causal, negmax[s % 2]).then_inc(maxed, 1)
                            if t.live(2):
                                if s == 0:
                                    dve.wait_ge(xmask_ready, t.item(2) + 1)
                                dve.wait_ge(xscores, t.item(2) * NG + (s + 1))
                                wait(dve, xturned, t.item(2) * NG + (s - 1))
                                settle(dve, settled)
                                masked(xprob[s % 2], XS, xmask[t.slot(2)], xnegmax[s % 2]).then_inc(xmaxed, 1)
                            if s == 0:
                                if t.live(-1):
                                    for n in (0, 1):
                                        dve.wait_ge(made[f"q{n}"], t.item(-1) + 1)
                                        nc.vector.tensor_scalar(qT[t.slot(-1)][:, 4 * n:4 * n + 4, :].rearrange("p c q -> p (c q)"),
                                                                JB[BANK[f"q{n}"]][:, :], DH ** -0.5, None, ALU.mult).then_inc(moved[f"q{n}"], 1)
                                normalise(t, s)
                            if s == 1:
                                cross_keys(t, 0)
                                normalise(t, s, lambda: cross_keys(t, 1))
                                norm_steps = norms_begin(t)
                                place_tokens(t)
                            if s == 2:
                                norms_end(t, norm_steps)
                                if t.live(-1):
                                    for n in (0, 1):
                                        dve.wait_ge(made[f"k{n}"], t.item(-1) + 1)
                                        nc.vector.tensor_copy(kD[t.slot(-1)][DH:P, 4 * n:4 * n + 4, P:2 * P],
                                                              JB[BANK[f"k{n}"]][DH:P, :].rearrange("p (c k) -> p c k", c=4)).then_inc(moved[f"k{n}"], 1)
                                normalise(t, s)
                            if s == 3:
                                if t.live(3):
                                    dve.wait_ge(made["route"], t.item(3) + 1)
                                if t.live(1):
                                    dve.wait_ge(made["xq"], t.item(1) + 1)
                                    for m in range(KC):
                                        last = nc.vector.tensor_scalar(xqT[t.slot(1)][:, m, :], JB[BANK["xq"]][:, m * P:(m + 1) * P], xbq_s[:, m:m + 1],
                                                                       XD ** -0.5, ALU.add, ALU.mult)
                                    last.then_inc(moved["xq"], 1)
                                top_two(t)
                                normalise(t, s)
                                if t.live(1):
                                    dve.wait_ge(made["xv"], t.item(1) + 1)
                                    for m in range(KC):
                                        for j in (0, 1):
                                            last = nc.vector.tensor_tensor(
                                                xvD[t.slot(1)][:, m, :, j, j * XD:(j + 1) * XD],
                                                JB[BANK["xv"]][:, m * P:(m + 1) * P].rearrange("p (h j d) -> p h j d", h=QUARTERS, j=2)[:, :, j, :],
                                                xbv_s[:, m * P:(m + 1) * P].rearrange("p (h j d) -> p h j d", h=QUARTERS, j=2)[:, :, j, :], ALU.add)
                                    last.then_inc(moved["xv"], 1)
                                if t.live(1):
                                    dve.wait_ge(mask_in[t.slot(1)], (t.turn(1) + 1) * 16)
                                    nc.vector.tensor_scalar(xmask[t.slot(1)][:, :], mask_s[t.slot(1)][:, :], 0.0, -BIG,
                                                            ALU.is_equal, ALU.mult).then_inc(xmask_ready, 1)
                                weigh(t)

                    pipeline(dve, iteration)

        with ExitStack() as two:
            def sb(name, shape, dt=F32):
                return tile(two, name, shape, dt)

            moe = sb("moe", [P, 3 * HALF, WCOL])
            moe_cols = moe[:, :, :].rearrange("p e n -> p (e n)")
            thirds = [moe[:, n * HALF:(n + 1) * HALF, :] for n in range(3)]

            tile_no = sb("tile_no", [P, NGRP, TA])
            expert_no = sb("expert_no", [P, NE])
            late = sb("late", [P, TA])
            counts_i = [sb(f"counts_i{i}", [P, NE], I32) for i in (0, 1)]
            ntiles = sb("ntiles", [P, NGRP, E])
            ends = [sb(f"ends{i}", [P, NGRP, E]) for i in (0, 1)]
            first_row = sb("first_row", [P, NE])
            passed = sb("passed", [P, NGRP, TA, E])
            passed_n = sb("passed_n", [P, NGRP, TA, E])
            tile_e, tile_j, tile_l = (sb(n, [P, NGRP, TA]) for n in ("tile_e", "tile_j", "tile_l"))
            tile_w = sb("tile_w", [P, TA])
            mix = [sb(f"mix{i}", [P, TA]) for i in range(3)]
            list_no = sb("list_no", [P, TA], I32)
            packs = [sb(f"packs{i}", [P, TA // PACK]) for i in (0, 1)]
            packed = sb("packed", [P, TA // PACK], I32)
            tabs = sb("tabs", [1, P * TA // PACK], I32)
            PLACES = 3 * HALF
            PLACE_BITS = PLACES.bit_length()
            assert PACK == 4 and PACK * PLACE_BITS <= 24
            lists = sb("lists", [P, TA, P], I32)
            lists_f = sb("lists_f", [P, TA, P])
            tokens = sb("tokens", [P, TA * P], I32)
            row = sb("row", [P, NB, SLOTS])
            match = [sb(f"match{i}", [P, NB, TOPK]) for i in (0, 1)]
            NQ = 4
            who = [sb(f"who{q}", [P, 1], I32) for q in range(NQ)]
            xg_s = [sb(f"xg{q}", [P, D]) for q in range(NQ)]
            xgT = [sb(f"xgT{q}", [P, KC, P]) for q in (0, 1)]
            gate_s = [sb(f"gate{q}", [P, HID]) for q in (0, 1)]
            h_s = [sb(f"h{q}", [P, HID]) for q in (0, 1)]
            hT_s = [sb(f"hT{q}", [P, P]) for q in (0, 1)]
            y_s = [sb(f"y{q}", [P, D]) for q in range(NQ)]
            want0 = [sb(f"want0_{p}", [P, TOPK], I32) for p in (0, 1)]
            rows0 = [sb(f"rows0_{p}", [P, TOPK, D]) for p in (0, 1)]
            x2c = [sb(f"x2c{p}", [P, D]) for p in (0, 1)]
            part = [sb(f"part{p}", [P, D]) for p in (0, 1)]
            acc0 = [sb(f"acc0_{p}", [P, D]) for p in (0, 1)]
            XB, GB, HB, YB = banks[0:2], banks[2:4], banks[4], banks[5:7]

            link, counted, tab_out, tab_in, lists_in, lists_fp, lists_t, tokens_ready = (
                sem(n) for n in ("link", "counted", "tab_out", "tab_in", "lists_in", "lists_fp", "lists_t", "tokens_ready"))
            moe_in = sem("moe_in")
            iotas, tabs_ready, looked = sem("iotas"), sem("tabs_ready"), sem("looked")
            who_ready = sem("who_ready")
            xg_in = [sem(f"xg_in{q}") for q in range(NQ)]
            xgt_made, xgt_in, gu_made, gate_in, h_in, ht_made, ht_in, y_made, y_in = (
                sem(n) for n in ("xgt_made", "xgt_in", "gu_made", "gate_in", "h_in", "ht_made", "ht_in", "y_made", "y_in"))
            y_out = [sem(f"y_out{q}") for q in range(NQ)]
            want0_ready, part_ready, acc0_ready = sem("want0_ready"), sem("part_ready"), sem("acc0_ready")
            rows0_in, x2c_in, acc0_out = ([sem(f"{n}{p}") for p in (0, 1)] for n in ("rows0_in", "x2c_in", "acc0_out"))

            GROUP_U = TILES // NQ
            FIRST_U = GROUP_U + 5
            COMBINE_U = NB // 2
            assert FIRST_U + COMBINE_U + 2 < 2 * GROUP_U
            LOOK = 2
            assert 2 + E // LOOK <= GROUP_U and LOOK * NGRP == NQ

            def tiles(eng, iteration, switch=None, look_up=None):

                def turn(u, combine, group=None, look_up=None):
                    for q in range(NQ):
                        iteration(When(u, q, NQ, 0, NT), When(u, q // 2, 2, 0, NB, 2 * FIRST_U + 2) if combine and q % 2 == 0 else None,
                                  {lag: int(NQ * u + q - lag >= TILES) if group is None else group for lag in (1, 3)})
                        if look_up:
                            look_up(u - 2, q)

                for u in range(2):
                    turn(u, False)
                with eng.Fori(2, 2 + E // LOOK) as u:
                    turn(u, False, 0, look_up)
                with eng.Fori(2 + E // LOOK, GROUP_U) as u:
                    turn(u, False, 0)
                turn(GROUP_U, False)
                if switch:
                    switch()
                with eng.Fori(GROUP_U + 1, FIRST_U) as u:
                    turn(u, False, 1)
                for u in range(FIRST_U, FIRST_U + 3):
                    turn(u, True)
                with eng.Fori(FIRST_U + 3, FIRST_U + COMBINE_U) as u:
                    turn(u, True, 1)
                for u in range(FIRST_U + COMBINE_U, 2 * GROUP_U + 1):
                    turn(u, True)

            def load_next(eng, n):
                g, half = divmod(n, 2)
                if n:
                    eng.wait_ge(moe_in, n * MOE_LOAD)
                load_experts(eng, thirds[(n + 1) % 3], half * HALF, *((g0, u0, d0), (g1, u1, d1))[g], moe_in)

            with nc.Block() as block:
                @block.sync
                def _(sp):
                    load_next(sp, 0)
                    sp.wait_ge(tabs_ready, 1)
                    sp.dma_start(tab_d.rearrange("(p a) -> p a", p=P), packed[:, :]).then_inc(tab_out, 16)
                    sp.wait_ge(tab_out, 16)
                    sp.dma_start(tabs[0:1, :], tab_d.rearrange("(o n) -> o n", o=1)).then_inc(tab_in, 16)
                    load_next(sp, 1)
                    load_next(sp, 2)

                    def iteration(t, b, g):
                        if t.live(3):
                            sp.wait_ge(y_in, t.item(3) + 1)
                            sp.dma_start(y_d[g[3]][bass.ds((t.item(3) - g[3] * TILES) * P, P), :], y_s[t.slot(3)][:, :]).then_inc(y_out[t.slot(3)], 16)
                        if b and b.live(0):
                            p = b.slot(0)
                            wait(sp, part_ready, b.item(2) + 1)
                            sp.dma_start(x2c[p][:, :], x2_d[bass.ds(b.item(0) * P, P), :]).then_inc(x2c_in[p], 16)
                        if b and b.live(2):
                            p = b.slot(2)
                            sp.wait_ge(acc0_ready, b.item(2) + 1)
                            sp.dma_start(acc_d[bass.ds(b.item(2) * P, P), :], acc0[p][:, :]).then_inc(acc0_out[p], 16)

                    tiles(sp, iteration)
                    for q in range(NQ):
                        sp.wait_ge(y_out[q], 16 * (NT // NQ))
                    for p in (0, 1):
                        sp.wait_ge(acc0_out[p], 16 * (NB // 2))

                @block.gpsimd
                def _(pool):
                    nc.gpsimd.iota(tile_no[:, :, :], pattern=[[-TILES, NGRP], [1, TA]], base=0, channel_multiplier=TA,
                                   allow_small_or_imprecise_dtypes=True).then_inc(iotas, 1)
                    nc.gpsimd.iota(expert_no[:, :], pattern=[[1, NE]], base=0, channel_multiplier=0,
                                   allow_small_or_imprecise_dtypes=True).then_inc(iotas, 1)
                    pool.wait_ge(tabs_ready, 1)
                    for a in range(TA):
                        nc.gpsimd.indirect_dma_start(
                            lists[:, a, :], None, list_d.rearrange("(r n) o -> r (n o)", n=P),
                            bass.IndirectOffsetOnAxis(ap=list_no[:, a:a + 1].bitcast(U32), axis=0)).then_inc(lists_in, 16)

                    def iteration(t, b, g):
                        if t.live(0):
                            q = t.slot(0)
                            pool.wait_ge(who_ready, t.item(0) + 1)
                            wait(pool, xgt_made, t.item(NQ) + 1)
                            settle(pool, settled)
                            nc.gpsimd.indirect_dma_start(
                                xg_s[q][:, :], None, x2_d[:, :],
                                bass.IndirectOffsetOnAxis(ap=who[q][:, :].bitcast(U32), axis=0)).then_inc(xg_in[q], 16)
                        if b and b.live(1):
                            p = b.slot(1)
                            if isinstance(b.u, int) and b.item(1) == 0:
                                for q in range(NQ):
                                    pool.wait_ge(y_out[q], 16 * GROUP_U)
                            pool.wait_ge(want0_ready, b.item(1) + 1)
                            wait(pool, acc0_ready, b.item(3) + 1)
                            settle(pool, settled)
                            for j in range(TOPK):
                                nc.gpsimd.indirect_dma_start(
                                    rows0[p][:, j, :], None, y_d[0][:, :],
                                    bass.IndirectOffsetOnAxis(ap=want0[p][:, j:j + 1].bitcast(U32), axis=0)).then_inc(rows0_in[p], 16)

                    tiles(pool, iteration)

                @block.tensor
                def _(pe):
                    nc.tensor.matmul(banks[7][:, 0:NE], ones_b[:, :], picked[:, :], start=True, stop=True).then_inc(counted, 1)
                    pe.wait_ge(lists_fp, 1)
                    for a in range(TA):
                        last = nc.tensor.transpose(banks[a // 4][:, (a % 4) * P:(a % 4 + 1) * P], lists_f[:, a, :], ident[:, :])
                    last.then_inc(lists_t, 1)
                    pe.wait_ge(tokens_ready, 1)
                    pe.wait_ge(tab_in, 16)

                    word_regs = {back: pe.alloc_register(f"word{back + 1}") for back in (-1, 0, 1)}
                    for back in (-1, 0):
                        pe.reg_mov(word_regs[back], 0)
                    pe.reg_load(word_regs[1], tabs[0:1, 0:1])

                    def place(t, lag):
                        word = pe.snap(word_regs[(t.p - lag) // PACK], min_val=0, max_val=2 ** (PACK * PLACE_BITS) - 1)
                        return ((word >> (t.slot(lag) * PLACE_BITS)) & (2 ** PLACE_BITS - 1)).with_bounds(min_val=0, max_val=PLACES - 1)

                    def iteration(t, b, g):
                        if t.p == 0:
                            for back in (-1, 0):
                                pe.reg_mov(word_regs[back], word_regs[back + 1])
                        if t.live(0):
                            q = t.slot(0)
                            pe.wait_ge(xg_in[q], (t.turn(0) + 1) * 16)
                            wait(pe, xgt_in, t.item(1))
                            for k in range(KC):
                                last = nc.tensor.transpose(XB[q % 2][:, k * P:(k + 1) * P], xg_s[q][:, k * P:(k + 1) * P], ident[:, :])
                            last.then_inc(xgt_made, 1)
                        if t.live(1):
                            q = t.slot(1)
                            at_place = place(t, 1)
                            pe.wait_ge(moe_in, ((at_place >> (HALF.bit_length() - 1)) + 3 * g[1]) * MOE_LOAD)
                            pe.wait_ge(xgt_in, t.item(1) + 1)
                            wait(pe, h_in, t.item(2))
                            for k in range(KC):
                                last = nc.tensor.matmul(GB[q % 2][:, 0:2 * HID], xgT[q % 2][:, k, :],
                                                        moe_cols[:, bass.ds(at_place * WCOL + k * 2 * HID, 2 * HID)], start=(k == 0), stop=(k == KC - 1))
                            last.then_inc(gu_made, 1)
                        if t.p == 2:
                            pe.reg_load(word_regs[1], tabs[0:1, bass.ds(t.u + 1, 1)])
                        if t.live(2):
                            q = t.slot(2)
                            pe.wait_ge(h_in, t.item(2) + 1)
                            wait(pe, ht_in, t.item(2))
                            nc.tensor.transpose(HB[:, 0:P], h_s[q % 2][:, :], ident[:, :]).then_inc(ht_made, 1)
                        if t.live(3):
                            q = t.slot(3)
                            first = pe.snap(place(t, 3) * WCOL + KC * 2 * HID)
                            pe.wait_ge(ht_in, t.item(3) + 1)
                            wait(pe, y_in, t.item(4))
                            nc.tensor.matmul(YB[q % 2][:, 0:D], hT_s[q % 2][:, :], moe_cols[:, bass.ds(first, D)],
                                             start=True, stop=True).then_inc(y_made, 1)

                    tiles(pe, iteration)

                @block.scalar
                def _(act):
                    def iteration(t, b, g):
                        if t.live(0):
                            q = t.slot(0)
                            act.wait_ge(xgt_made, t.item(0) + 1)
                            wait(act, gu_made, t.item(1))
                            nc.scalar.copy(xgT[q % 2][:, :, :].rearrange("p k t -> p (k t)"), XB[q % 2][:, 0:D]).then_inc(xgt_in, 1)
                        if t.live(2):
                            q = t.slot(2)
                            act.wait_ge(ht_made, t.item(2) + 1)
                            nc.scalar.copy(hT_s[q % 2][:, :], HB[:, 0:P]).then_inc(ht_in, 1)
                        if t.live(1):
                            q = t.slot(1)
                            act.wait_ge(gu_made, t.item(1) + 1)
                            nc.scalar.activation(gate_s[q % 2][:, :], GB[q % 2][:, 0:HID], ACT.Silu).then_inc(gate_in, 1)

                    def switch():
                        act.wait_ge(y_made, TILES)
                        load_next(act, 3)

                    tiles(act, iteration, switch)

                @block.vector
                def _(dve):
                    made = [0]

                    def linked(instruction):
                        made[0] += 1
                        instruction.then_inc(link, 1)
                        dve.wait_ge(link, made[0])

                    v = nc.vector
                    dve.wait_ge(counted, 1)
                    dve.wait_ge(iotas, 2)
                    linked(v.tensor_scalar(counts_i[0][:, :], banks[7][:, 0:NE], float(P - 1), None, ALU.add))
                    linked(v.tensor_single_scalar(counts_i[1][:, :], counts_i[0][:, :], P.bit_length() - 1, op=ALU.arith_shift_right))
                    linked(v.tensor_copy(ntiles[:, :, :].rearrange("p g e -> p (g e)"), counts_i[1][:, :]))
                    linked(v.tensor_copy(ends[0][:, :, :], ntiles[:, :, :]))
                    d, n = 1, 0
                    while d < E:
                        linked(v.tensor_copy(ends[1 - n][:, :, 0:d], ends[n][:, :, 0:d]))
                        linked(v.tensor_tensor(ends[1 - n][:, :, d:E], ends[n][:, :, d:E], ends[n][:, :, 0:E - d], ALU.add))
                        d, n = 2 * d, 1 - n
                    end = ends[n]
                    for g in range(NGRP):
                        linked(v.tensor_tensor(first_row[:, g * E:(g + 1) * E], end[:, g, :], ntiles[:, g, :], ALU.subtract))
                        linked(v.tensor_scalar(first_row[:, g * E:(g + 1) * E], first_row[:, g * E:(g + 1) * E], float(P), None, ALU.mult))
                    for g in range(NGRP):
                        linked(v.tensor_tensor(passed[:, g, :, :], spread(end[:, g, :], 1, TA), spread(tile_no[:, g, :], 2, E), ALU.is_le))
                        linked(v.tensor_tensor(passed_n[:, g, :, :], passed[:, g, :, :], spread(ntiles[:, g, :], 1, TA), ALU.mult))
                        linked(v.tensor_reduce(tile_e[:, g, :], passed[:, g, :, :], AX.X, ALU.add))
                        linked(v.tensor_reduce(tile_j[:, g, :], passed_n[:, g, :, :], AX.X, ALU.add))
                    linked(v.tensor_tensor(tile_j[:, :, :], tile_no[:, :, :], tile_j[:, :, :], ALU.subtract))
                    linked(v.tensor_scalar(tile_j[:, :, :], tile_j[:, :, :], float(N // P - 1), 0.0, ALU.min, ALU.max))
                    linked(v.tensor_scalar(tile_e[:, :, :], tile_e[:, :, :], float(E - 1), None, ALU.min))
                    linked(v.scalar_tensor_tensor(tile_l[:, :, :], tile_e[:, :, :], float(N // P), tile_j[:, :, :], ALU.mult, ALU.add))
                    linked(v.tensor_scalar(late[:, :], tile_no[:, 0, :], float(TILES), None, ALU.is_ge))
                    linked(v.tensor_scalar(mix[0][:, :], tile_l[:, 1, :], float(E * N // P), None, ALU.add))
                    linked(v.tensor_tensor(mix[1][:, :], mix[0][:, :], tile_l[:, 0, :], ALU.subtract))
                    linked(v.tensor_tensor(mix[2][:, :], mix[1][:, :], late[:, :], ALU.mult))
                    linked(v.tensor_tensor(list_no[:, :], mix[2][:, :], tile_l[:, 0, :], ALU.add))
                    linked(v.tensor_scalar(mix[0][:, :], tile_e[:, 0, :], float(HALF), None, ALU.add))
                    linked(v.tensor_tensor(mix[1][:, :], tile_e[:, 1, :], mix[0][:, :], ALU.subtract))
                    linked(v.tensor_tensor(mix[2][:, :], mix[1][:, :], late[:, :], ALU.mult))
                    linked(v.tensor_tensor(tile_w[:, :], mix[2][:, :], mix[0][:, :], ALU.add))
                    quads = tile_w[:, :].rearrange("p (w n) -> p w n", n=PACK)
                    linked(v.scalar_tensor_tensor(packs[0][:, :], quads[:, :, 3], float(2 ** PLACE_BITS), quads[:, :, 2], ALU.mult, ALU.add))
                    linked(v.scalar_tensor_tensor(packs[1][:, :], packs[0][:, :], float(2 ** PLACE_BITS), quads[:, :, 1], ALU.mult, ALU.add))
                    v.scalar_tensor_tensor(packed[:, :], packs[1][:, :], float(2 ** PLACE_BITS), quads[:, :, 0], ALU.mult, ALU.add).then_inc(tabs_ready, 1)
                    v.tensor_copy(row[:, :, :], rank[:, :, :]).then_inc(looked, 1)
                    dve.wait_ge(lists_in, 16 * TA)
                    v.tensor_copy(lists_f[:, :, :], lists[:, :, :]).then_inc(lists_fp, 1)
                    dve.wait_ge(lists_t, 1)
                    for a in range(TA):
                        last = v.tensor_copy(tokens[:, :].rearrange("n (p a) -> n p a", a=TA)[:, :, a], banks[a // 4][:, (a % 4) * P:(a % 4 + 1) * P])
                    last.then_inc(tokens_ready, 1)
                    dve.wait_ge(tokens_ready, 1)

                    AHEAD = 3

                    def name_tokens(t, lag):
                        if t.live(lag):
                            q = t.slot(lag)
                            wait(dve, xg_in[q], t.turn(lag) * 16)
                            v.tensor_copy(who[q][:, :], tokens[:, bass.ds(t.item(lag), 1)]).then_inc(who_ready, 1)

                    def iteration(t, b, g):
                        name_tokens(t, -AHEAD)
                        if b and b.live(-1):
                            p = b.slot(-1)
                            wait(dve, rows0_in[p], b.turn(-1) * (16 * TOPK))
                            v.tensor_copy(want0[p][:, :], row_i[:, bass.ds(b.item(-1), 1), 0:TOPK].rearrange("p o s -> p (o s)")).then_inc(want0_ready, 1)
                        if t.live(3):
                            q = t.slot(3)
                            dve.wait_ge(y_made, t.item(3) + 1)
                            wait(dve, y_out[q], t.turn(3) * 16)
                            v.tensor_copy(y_s[q][:, :], YB[q % 2][:, 0:D]).then_inc(y_in, 1)
                        if t.live(1):
                            q = t.slot(1)
                            dve.wait_ge(gate_in, t.item(1) + 1)
                            wait(dve, ht_made, t.item(2))
                            v.tensor_tensor(h_s[q % 2][:, :], gate_s[q % 2][:, :], GB[q % 2][:, HID:2 * HID], ALU.mult).then_inc(h_in, 1)
                        if b and b.live(1):
                            p = b.slot(1)
                            dve.wait_ge(rows0_in[p], (b.turn(1) + 1) * (16 * TOPK))
                            dve.wait_ge(x2c_in[p], (b.turn(1) + 1) * 16)
                            wait(dve, acc0_ready, b.item(3) + 1)
                            v.scalar_tensor_tensor(part[p][:, :], rows0[p][:, 0, :], weight0(b, 0), x2c[p][:, :], ALU.mult, ALU.add).then_inc(part_ready, 1)
                        if b and b.live(1):
                            p = b.slot(1)
                            dve.wait_ge(part_ready, b.item(1) + 1)
                            wait(dve, acc0_out[p], b.turn(1) * 16)
                            v.scalar_tensor_tensor(acc0[p][:, :], rows0[p][:, 1, :], weight0(b, 1), part[p][:, :], ALU.mult, ALU.add).then_inc(acc0_ready, 1)

                    def weight0(b, j):
                        return weight[:, bass.ds(b.item(1), 1), j:j + 1].rearrange("p o s -> p (o s)")

                    def look_up(n, q):
                        i, g = divmod(q, NGRP)
                        own = slice(g * TOPK, (g + 1) * TOPK)
                        e = n * LOOK + (g * E + i)
                        before = n * (2 * NQ) + (2 * q + 1)
                        dve.wait_ge(looked, before)
                        v.tensor_scalar(match[g][:, :, :], expert[:, :, own], expert_no[:, bass.ds(e, 1)], first_row[:, bass.ds(e, 1)],
                                        ALU.is_equal, ALU.mult).then_inc(looked, 1)
                        dve.wait_ge(looked, before + 1)
                        v.tensor_tensor(row[:, :, own], row[:, :, own], match[g][:, :, :], ALU.add).then_inc(looked, 1)

                    def row_numbers():
                        dve.wait_ge(looked, 2 * NE + 1)
                        v.tensor_copy(row_i[:, :, :], row[:, :, :]).then_inc(looked, 1)
                        dve.wait_ge(looked, 2 * NE + 2)

                    for n in range(AHEAD):
                        name_tokens(at(n, NQ, 0, NT), 0)
                    tiles(dve, iteration, row_numbers, look_up)

        with ExitStack() as three:
            def sb(name, shape, dt=F32):
                return tile(three, name, shape, dt)

            QUAD = 4
            QUADS = NB // QUAD
            halves = [(h, q) for h in (0, 1) for q in range(QUAD)]
            want = {k: sb(f"want{k[0]}{k[1]}", [P, TOPK], I32) for k in halves}
            rows1 = {k: sb(f"rows{k[0]}{k[1]}", [P, TOPK, D]) for k in halves}
            sum0 = {k: sb(f"sum0{k[0]}{k[1]}", [P, D]) for k in halves}
            acc = [sb(f"acc{q}", [P, D]) for q in range(QUAD)]
            o_s = {k: sb(f"o{k[0]}{k[1]}", [P, D]) for k in halves}
            st4, mv4 = sb("st4", [P, QUAD, 6]), sb("mv4", [P, QUAD, 2])
            ve, bits, rstd, ya, yb = (sb(n, [P, QUAD]) for n in ("ve", "bits", "rstd", "ya", "yb"))
            rows_in = {k: sem(f"rows_in{k[0]}{k[1]}") for k in halves}
            sum0_in = {k: sem(f"sum0_in{k[0]}{k[1]}") for k in halves}
            out_done = {k: sem(f"out_done{k[0]}{k[1]}") for k in halves}
            want_ready, rows_used, o_ready, step_done = (sem(n) for n in ("want_ready", "rows_used", "o_ready", "step_done"))

            def quads(eng, body):
                for h in (0, 1):
                    body(h, h, 0)
                with eng.Fori(1, QUADS // 2 - 1) as u:
                    for h in (0, 1):
                        body(u * 2 + h, h, u)
                for h in (0, 1):
                    body(QUADS - 2 + h, h, QUADS // 2 - 1)

            with nc.Block() as block:
                @block.sync
                def _(sp):
                    def body(n, h, u):
                        for q in range(QUAD):
                            wait(sp, rows_used, (n - 2) * QUAD + (q + 1))
                            sp.dma_start(sum0[h, q][:, :], acc_d[bass.ds((n * QUAD + q) * P, P), :]).then_inc(sum0_in[h, q], 16)

                    quads(sp, body)

                @block.gpsimd
                def _(pool):
                    def body(n, h, u):
                        for q in range(QUAD):
                            pool.wait_ge(want_ready, n * QUAD + (q + 1))
                            wait(pool, rows_used, (n - 2) * QUAD + (q + 1))
                            settle(pool, settled)
                            for j in range(TOPK):
                                nc.gpsimd.indirect_dma_start(
                                    rows1[h, q][:, j, :], None, y_d[1][:, :],
                                    bass.IndirectOffsetOnAxis(ap=want[h, q][:, j:j + 1].bitcast(U32), axis=0)).then_inc(rows_in[h, q], 16)

                    quads(pool, body)

                @block.scalar
                def _(act):
                    def body(n, h, u):
                        for q in range(QUAD):
                            act.wait_ge(o_ready, n * QUAD + (q + 1))
                            act.dma_start(out[bass.ds(n * QUAD + q, 1), :, :].rearrange("o p d -> (o p) d"), o_s[h, q][:, :]).then_inc(out_done[h, q], 16)

                    quads(act, body)
                    for k in halves:
                        act.wait_ge(out_done[k], 16 * (QUADS // 2))

                @block.vector
                def _(dve):
                    v = nc.vector

                    def name_rows(n, h, u):
                        for q in range(QUAD):
                            wait(dve, rows_in[h, q], u * (16 * TOPK))
                            v.tensor_copy(want[h, q][:, :], row_i[:, bass.ds(n * QUAD + q, 1), SLOTS - TOPK:SLOTS].rearrange("p o s -> p (o s)")).then_inc(want_ready, 1)

                    def body(n, h, u):
                        if not (isinstance(u, int) and u == QUADS // 2 - 1 and h == 1):
                            name_rows(n + 1, 1 - h, u + h)
                        steps = Steps(dve, step_done, STEPS, n)
                        for j in range(TOPK):
                            for q in range(QUAD):
                                if j == 0:
                                    dve.wait_ge(rows_in[h, q], (u + 1) * (16 * TOPK))
                                    dve.wait_ge(sum0_in[h, q], (u + 1) * 16)
                                    wait(dve, o_ready, (n - 1) * QUAD + (q + 1))
                                else:
                                    steps.need((j - 1) * QUAD + q + 1)
                                w = weight[:, bass.ds(n * QUAD + q, 1), SLOTS - TOPK + j:SLOTS - TOPK + j + 1].rearrange("p o s -> p (o s)")
                                last = v.scalar_tensor_tensor(acc[q][:, :], rows1[h, q][:, j, :], w, (acc[q] if j else sum0[h, q])[:, :],
                                                              ALU.mult, ALU.add)
                                if j == TOPK - 1:
                                    last.then_inc(rows_used, 1)
                                else:
                                    steps.done(last)
                        for q in range(QUAD):
                            dve.wait_ge(rows_used, n * QUAD + (q + 1))
                            steps.done(v.bn_stats(st4[:, q, :], acc[q][:, :]))
                        for q in range(QUAD):
                            steps.need((TOPK - 1) * QUAD + q + 1)
                            settle(dve, settled)
                            steps.done(v.bn_aggr(mv4[:, q, :], st4[:, q, :]))
                        steps.need()
                        chain = (mv4[:, :, 1], ve[:, :], bits[:, :], rstd[:, :], ya[:, :], yb[:, :])
                        rsqrt_begin(steps, chain)
                        rsqrt_end(steps, chain)
                        steps.need()
                        for q in range(QUAD):
                            wait(dve, out_done[h, q], u * 16)
                            v.tensor_scalar(o_s[h, q][:, :], acc[q][:, :], mv4[:, q, 0:1], rstd[:, q:q + 1], ALU.subtract, ALU.mult).then_inc(o_ready, 1)

                    STEPS = (TOPK + 1) * QUAD + RSQRT_STEPS
                    name_rows(0, 0, 0)
                    quads(dve, body)


_INS = ["xT", "x", "cT", "mask", "wq", "wk", "wv", "wo", "xwq", "xbq", "xwk", "xbk", "xwv", "xbv", "xwo", "xbo",
        "r0", "g0", "u0", "d0", "r1", "g1", "u1", "d1"]


def kernel(x, ctx_1024, mask_BxSxS2_ik1, L0_attn_w_q, L0_attn_w_k, L0_attn_w_v, L0_attn_w_o, L0_xattn_Wq, L0_xattn_bq,
           L0_xattn_Wk, L0_xattn_bk, L0_xattn_Wv, L0_xattn_bv, L0_xattn_Wo, L0_xattn_bo, L0_ffn_router_w0, L0_ffn_wg0,
           L0_ffn_wu0, L0_ffn_wd0, L0_ffn_router_w1, L0_ffn_wg1, L0_ffn_wu1, L0_ffn_wd1):
    import numpy as np
    import concourse.bacc as bacc
    from concourse.bass_utils import run_bass_kernel_spmd

    def by_partition(w):
        w = np.asarray(w)
        return np.ascontiguousarray(w.reshape(-1, P, w.shape[1]).transpose(1, 0, 2).reshape(P, -1))

    def tokens_last(a):
        a = np.asarray(a)
        return np.ascontiguousarray(a.reshape(a.shape[0], P, KC, P).transpose(0, 3, 2, 1).reshape(a.shape[0], P, KC * P))

    def flat_t(w):
        return np.asarray(w).reshape(HD, D).T

    def column(b):
        return np.ascontiguousarray(np.asarray(b).reshape(KC, P).T)

    def one_row(b):
        return np.asarray(b).reshape(1, D)

    arrays = dict(
        xT=tokens_last(x), x=np.asarray(x), cT=tokens_last(ctx_1024), mask=np.asarray(mask_BxSxS2_ik1),
        wq=by_partition(flat_t(L0_attn_w_q)), wk=by_partition(flat_t(L0_attn_w_k)), wv=by_partition(flat_t(L0_attn_w_v)),
        wo=by_partition(L0_attn_w_o),
        xwq=by_partition(np.asarray(L0_xattn_Wq).T), xbq=column(L0_xattn_bq), xwk=by_partition(np.asarray(L0_xattn_Wk).T),
        xbk=column(L0_xattn_bk), xwv=by_partition(np.asarray(L0_xattn_Wv).T), xbv=one_row(L0_xattn_bv),
        xwo=by_partition(np.asarray(L0_xattn_Wo).T), xbo=one_row(L0_xattn_bo),
        r0=np.asarray(L0_ffn_router_w0), g0=np.asarray(L0_ffn_wg0), u0=np.asarray(L0_ffn_wu0), d0=np.asarray(L0_ffn_wd0),
        r1=np.asarray(L0_ffn_router_w1), g1=np.asarray(L0_ffn_wg1), u1=np.asarray(L0_ffn_wu1), d1=np.asarray(L0_ffn_wd1))
    nc = bacc.Bacc("TRN2", target_bir_lowering=False, num_devices=1)
    aps = [nc.dram_tensor(n, arrays[n].shape, mybir.dt.from_np(arrays[n].dtype), kind="ExternalInput").ap() for n in _INS]
    out = nc.dram_tensor("out", tuple(x.shape), F32, kind="ExternalOutput").ap()
    decoder_layer(nc, *aps, out)
    result = run_bass_kernel_spmd(nc, [arrays], core_ids=[0])
    return result.results[0]["out"]
```
